# Optimizing a Trainium2 kernel written in Bass

```python
import numpy as np
import jax
import jax.numpy as jnp

def _softmax(x, axis=-1):
    return jax.nn.softmax(x, axis=axis)

def _gelu(x):
    return jax.nn.gelu(x, approximate=True)

def _silu(x):
    return jax.nn.silu(x)

def _sigmoid(x):
    return jax.nn.sigmoid(x)

def _layernorm(x, axis=-1, eps=1e-05):
    m = jnp.mean(x, axis=axis, keepdims=True)
    v = jnp.var(x, axis=axis, keepdims=True)
    return (x - m) / jnp.sqrt(v + eps)

def _scatter_add(tgt, idx, src, axis=0):
    return tgt.at[idx].add(src)

def _segment_sum(src, seg, n):
    return jax.ops.segment_sum(src, seg, n)
kernel_name = 'mk_seq_postln_d1_jaxref_r8_22b81a'

def setup_inputs(seed: int=0):
    np.random.seed(seed)
    _w = jnp.asarray

    def _L0_attn_setup():
        import jax, jax.numpy as jnp
        import numpy as np
        DIM = 512
        N_HEADS = 32
        N_KV_HEADS = 8
        HEAD_DIM = DIM // N_HEADS
        N_REP = N_HEADS // N_KV_HEADS
        ROPE_BASE = 500000.0
        B, S = (2, 256)

        def _rope_cos_sin(seq_len, head_dim):
            inv_freq = 1.0 / ROPE_BASE ** (jnp.arange(0, head_dim, 2, dtype=jnp.float32) / head_dim)
            t = jnp.arange(seq_len, dtype=jnp.float32)
            freqs = jnp.outer(t, inv_freq)
            return (jnp.cos(freqs), jnp.sin(freqs))

        def _apply_rope(x, cos, sin):
            half = x.shape[-1] // 2
            x1, x2 = (x[..., :half], x[..., half:])
            return jnp.concatenate([x1 * cos - x2 * sin, x2 * cos + x1 * sin], axis=-1)
        key = jax.random.key(seed)
        k1, k2, k3 = jax.random.split(key, 3)
        x = jax.random.normal(k1, (B, S, DIM), dtype=jnp.float32)
        qkv_out = (N_HEADS + 2 * N_KV_HEADS) * HEAD_DIM
        w_qkv = jax.random.normal(k2, (qkv_out, DIM), dtype=jnp.float32) * DIM ** (-0.5)
        w_o = jax.random.normal(k3, (DIM, DIM), dtype=jnp.float32) * DIM ** (-0.5)
        return {'x': x, 'w_qkv': w_qkv, 'w_o': w_o}
    _L0_attn_in = _L0_attn_setup()

    def _L0_ffn_setup():
        import jax, jax.numpy as jnp
        import numpy as np
        B, S, D, O, E, R = (4, 256, 512, 512, 8, 16)
        SCALING = 32.0 / 16.0
        MAX_THRESHOLD = 0.125
        key = jax.random.key(seed)
        ks = jax.random.split(key, 8)
        return {'x': jax.random.normal(ks[0], (B, S, D), jnp.float32), 'W_base': jax.random.normal(ks[1], (O, D), jnp.float32) * (1.0 / np.sqrt(D)), 'b_base': jax.random.normal(ks[2], (O,), jnp.float32) * 0.02, 'W_gate': jax.random.normal(ks[3], (E, D), jnp.float32) * (1.0 / np.sqrt(D)), 'W_thr': jax.random.normal(ks[4], (D,), jnp.float32) * (1.0 / np.sqrt(D)), 'b_thr': jax.random.normal(ks[5], (1,), jnp.float32) * 0.02, 'A_w': jax.random.normal(ks[6], (E, R, D), jnp.float32) * (1.0 / np.sqrt(D)), 'B_w': jax.random.normal(ks[7], (E, O, R), jnp.float32) * (1.0 / np.sqrt(R))}
    _L0_ffn_in = _L0_ffn_setup()
    _d = {'L0_attn_x': _L0_attn_in['x'], 'L0_attn_w_qkv': _L0_attn_in['w_qkv'], 'L0_attn_w_o': _L0_attn_in['w_o'], 'L0_ffn_W_base': _L0_ffn_in['W_base'], 'L0_ffn_b_base': _L0_ffn_in['b_base'], 'L0_ffn_W_gate': _L0_ffn_in['W_gate'], 'L0_ffn_W_thr': _L0_ffn_in['W_thr'], 'L0_ffn_b_thr': _L0_ffn_in['b_thr'], 'L0_ffn_A_w': _L0_ffn_in['A_w'], 'L0_ffn_B_w': _L0_ffn_in['B_w']}
    _x0 = _d['L0_attn_x']
    _d['L0_attn_x'] = jax.random.normal(jax.random.fold_in(jax.random.key(seed), 1), (4, 256, 512), dtype=_x0.dtype)
    del _x0
    return _d

def reference(L0_attn_x, L0_attn_w_qkv, L0_attn_w_o, L0_ffn_W_base, L0_ffn_b_base, L0_ffn_W_gate, L0_ffn_W_thr, L0_ffn_b_thr, L0_ffn_A_w, L0_ffn_B_w):

    def _L0_attn_ref(x, w_qkv, w_o):
        import jax, jax.numpy as jnp
        import numpy as np
        DIM = 512
        N_HEADS = 32
        N_KV_HEADS = 8
        HEAD_DIM = DIM // N_HEADS
        N_REP = N_HEADS // N_KV_HEADS
        ROPE_BASE = 500000.0
        B, S = (2, 256)

        def _rope_cos_sin(seq_len, head_dim):
            inv_freq = 1.0 / ROPE_BASE ** (jnp.arange(0, head_dim, 2, dtype=jnp.float32) / head_dim)
            t = jnp.arange(seq_len, dtype=jnp.float32)
            freqs = jnp.outer(t, inv_freq)
            return (jnp.cos(freqs), jnp.sin(freqs))

        def _apply_rope(x, cos, sin):
            half = x.shape[-1] // 2
            x1, x2 = (x[..., :half], x[..., half:])
            return jnp.concatenate([x1 * cos - x2 * sin, x2 * cos + x1 * sin], axis=-1)
        batch, seq_len, _ = x.shape
        qkv = jnp.einsum('bsd,od->bso', x, w_qkv)
        q_size = N_HEADS * HEAD_DIM
        kv_size = N_KV_HEADS * HEAD_DIM
        q = qkv[:, :, :q_size].reshape(batch, seq_len, N_HEADS, HEAD_DIM).transpose(0, 2, 1, 3)
        k = qkv[:, :, q_size:q_size + kv_size].reshape(batch, seq_len, N_KV_HEADS, HEAD_DIM).transpose(0, 2, 1, 3)
        v = qkv[:, :, q_size + kv_size:].reshape(batch, seq_len, N_KV_HEADS, HEAD_DIM).transpose(0, 2, 1, 3)
        cos, sin = _rope_cos_sin(seq_len, HEAD_DIM)
        cos = cos[None, None]
        sin = sin[None, None]
        q = _apply_rope(q, cos, sin)
        k = _apply_rope(k, cos, sin)
        k = jnp.repeat(k, N_REP, axis=1)
        v = jnp.repeat(v, N_REP, axis=1)
        scale = 1.0 / np.sqrt(HEAD_DIM).astype(np.float32)
        scores = jnp.einsum('bhqd,bhkd->bhqk', q, k) * scale
        causal = jnp.tril(jnp.ones((seq_len, seq_len), dtype=bool))
        scores = jnp.where(causal, scores, jnp.finfo(scores.dtype).min)
        attn = jax.nn.softmax(scores, axis=-1)
        out = jnp.einsum('bhqk,bhkd->bhqd', attn, v)
        out = out.transpose(0, 2, 1, 3).reshape(batch, seq_len, N_HEADS * HEAD_DIM)
        return jnp.einsum('bso,do->bsd', out, w_o)

    def _L0_ffn_ref(x, W_base, b_base, W_gate, W_thr, b_thr, A_w, B_w):
        import jax, jax.numpy as jnp
        import numpy as np
        B, S, D, O, E, R = (4, 256, 512, 512, 8, 16)
        SCALING = 32.0 / 16.0
        MAX_THRESHOLD = 0.125
        base = jnp.einsum('bsd,od->bso', x, W_base) + b_base
        xf = x.reshape(-1, D)
        gate = jax.nn.softmax(xf @ W_gate.T, axis=-1)
        thr = jax.nn.sigmoid(xf @ W_thr + b_thr[0]) * MAX_THRESHOLD
        adapted = gate - thr[:, None]
        selected = (adapted >= 0).astype(x.dtype)
        w = adapted * selected
        wsum = jnp.sum(w, axis=-1, keepdims=True)
        wsum = jnp.where(wsum == 0, jnp.ones_like(wsum), wsum)
        w = w / wsum
        h = jnp.einsum('nd,erd->ner', xf, A_w)
        moe = jnp.einsum('ner,ne,eor->no', h, w, B_w) * SCALING
        return base + moe.reshape(base.shape)
    x = L0_attn_x
    x = _layernorm(x + _L0_attn_ref(x, L0_attn_w_qkv, L0_attn_w_o), axis=-1)
    x = _layernorm(x + _L0_ffn_ref(x, L0_ffn_W_base, L0_ffn_b_base, L0_ffn_W_gate, L0_ffn_W_thr, L0_ffn_b_thr, L0_ffn_A_w, L0_ffn_B_w), axis=-1)
    return x

_drawn_inputs = setup_inputs


def setup_inputs(seed=0):
    import zlib

    import numpy as np

    out = dict(_drawn_inputs(seed))
    spreads = {}
    factors = {'L0_ffn_b_base': 5.53}
    for name, (base, spread) in spreads.items():
        noise = np.random.default_rng([zlib.crc32(name.encode()), seed]).standard_normal(out[name].shape)
        drawn = base * np.exp(spread * noise) if base else spread * noise
        out[name] = jnp.asarray(drawn.astype(out[name].dtype))
    for name, factor in factors.items():
        out[name] = (out[name] * factor).astype(out[name].dtype)
    return out
```

```python
from contextlib import ExitStack
import math

import concourse.bass as bass
from concourse import mybir

F32 = mybir.dt.float32
F32R = mybir.dt.float32r
BF16 = mybir.dt.bfloat16
F16 = mybir.dt.float16
ALU = mybir.AluOpType
ACT = mybir.ActivationFunctionType
AX = mybir.AxisListType

P = 128
B, S, D = 4, 256, 512
NT = S // P
KC = D // P
G, R, DH = 8, 4, 16
H = G * R
QK = (R + 1) * P
QKV = QK + G * DH
E, LR = 8, 16
AG = E * LR + E + 2
EPS = 1e-5
SCALING = 2.0
MAX_THRESHOLD = 0.125
SCALE = 1.0 / math.sqrt(DH)
LIFT = math.log(1024.0) / SCALE
Q_PARTS = (0, 1, 0, 1, 2, 0)
K_PARTS = (0, 0, 1, 1, 0, 2)
ROWS = 16 * len(Q_PARTS)
VC = 3 * DH + 1
UNITS = B * G
PCOLS = R * S + R * P
MASKED = -1e37
V_RING = 3

LAG_ST, LAG_SPLIT, LAG_PV = 6, 7, 8
STEPS = UNITS + 2 * G


def build(nc, xT, x, wqkv, wo, wb, ag, bw, bbase, bthr, tab, out):
    ctx = ExitStack()
    with ctx:
        def sb(name, shape, dt):
            return ctx.enter_context(nc.sbuf_tensor(name, shape, dt))

        def sem(name):
            return ctx.enter_context(nc.semaphore(name))

        raw = sb("raw", [P, 3, QKV], F32)
        wq_hi, wq_lo = (sb(n, [P, KC, QKV], F32R) for n in ("wq_hi", "wq_lo"))
        wo_hi, wo_lo = (sb(n, [P, KC, D], F32R) for n in ("wo_hi", "wo_lo"))
        wb_hi, wb_lo = (sb(n, [P, KC, D], F32R) for n in ("wb_hi", "wb_lo"))
        ag_hi, ag_lo = (sb(n, [P, KC, AG], F32R) for n in ("ag_hi", "ag_lo"))
        bw_hi, bw_lo = (sb(n, [P, D], F32R) for n in ("bw_hi", "bw_lo"))
        xT_raw = sb("xT_raw", [P, KC, S], F32)
        xT_hi, xT_lo = (sb(n, [P, KC, S], F32R) for n in ("xT_hi", "xT_lo"))
        x_tok = sb("x_tok", [P, NT, D], F32)
        swapped = sb("swapped", [P, 2 * S], F32)
        roped_cos = sb("roped_cos", [P, 2 * S], F32)
        qk = sb("qk", [P, R + 1, S], F32)
        part = [sb(f"part{i}", [P, R + 1, S], BF16) for i in range(3)]
        q_aug = [sb(f"q_aug{i}", [ROWS + 2, H, S], BF16) for i in range(2)]
        k_aug = [sb(f"k_aug{i}", [ROWS + 2, G, S], BF16) for i in range(2)]
        v_aug = sb("v_aug", [P, V_RING, NT, G, VC], BF16)
        v_rest = sb("v_rest", [P, NT, G, DH], F32)
        neg_max = sb("neg_max", [P, 2, NT, 4 * R], F32)
        m_part = [sb(f"m_part{i}", [NT * 4 * R, P], BF16) for i in range(2)]
        prob = sb("prob", [P, 2, PCOLS], F32)
        p1 = sb("p1", [P, 2, PCOLS], F16)
        p2 = sb("p2", [P, 2, PCOLS], F16)
        o_sum = sb("o_sum", [P, 2, NT * R, DH], F32)
        o_inv = sb("o_inv", [P, 2, NT * R], F32)
        attn = sb("attn", [P, NT, D], F32)
        aT_hi, aT_lo = (sb(n, [P, NT, KC, P], F32R) for n in ("aT_hi", "aT_lo"))
        s_buf = sb("s_buf", [P, NT, D], F32)
        y_buf = sb("y_buf", [P, NT, D], F32)
        stats = sb("stats", [P, NT, 6], F32)
        mean_var = sb("mean_var", [P, NT, 2], F32)
        var_eps = sb("var_eps", [P, NT], F32)
        rstd = sb("rstd", [P, NT], F32)
        h_raw = sb("h_raw", [P, NT, AG], F32)
        neg_top = sb("neg_top", [P, NT], F32)
        gate_e = sb("gate_e", [P, NT, E], F32)
        gate_c = sb("gate_c", [P, 2, NT], F32)
        gate_r = sb("gate_r", [P, 2, NT], F32)
        gate_t = sb("gate_t", [P, NT], F32)
        gate_w = sb("gate_w", [P, NT, E], F32)
        w_sum = sb("w_sum", [P, NT], F32)
        w_inv = sb("w_inv", [P, NT], F32)
        h_w = sb("h_w", [P, NT, E * LR], F32)
        hT_hi, hT_lo = (sb(n, [P, NT, P], F32R) for n in ("hT_hi", "hT_lo"))
        ident = sb("ident", [P, P], F32)
        ident_b = sb("ident_b", [P, P], BF16)
        mask_b = sb("mask_b", [P, P], BF16)
        b_row = sb("b_row", [P, D], F32)
        b_thr = sb("b_thr", [P, 1], F32)
        tables = sb("tables", [P, 2, S], F32)
        half = sb("half", [P, NT], F32)

        score = [ctx.enter_context(nc.psum_tensor(f"score{i}", [P, 512], F32)) for i in range(2)]
        st_a = ctx.enter_context(nc.psum_tensor("st_a", [P, 1024], F32))
        st_b = ctx.enter_context(nc.psum_tensor("st_b", [P, 512], F32))
        o_ps = ctx.enter_context(nc.psum_tensor("o_ps", [P, 512], F32))
        acc = ctx.enter_context(nc.psum_tensor("acc", [P, 512], F32))
        turn = ctx.enter_context(nc.psum_tensor("turn", [P, 512], F32))
        o_view = o_ps[:, 0:NT * R * VC].rearrange("p (n c) -> p n c", c=VC)

        raw_in = [sem(f"raw_in{i}") for i in range(3)]
        raw_hi = sem("raw_hi")
        raw_lo = sem("raw_lo")
        xT_in, x_in, small_in = sem("xT_in"), sem("x_in"), sem("small_in")
        xT_hi_done, xT_lo_done = sem("xT_hi_done"), sem("xT_lo_done")
        consts, ones = sem("consts"), sem("ones")
        acc_full, acc_free = sem("acc_full"), sem("acc_free")
        turn_full, turn_free = sem("turn_full"), sem("turn_free")
        swap_done, rope_done, rest_done = sem("swap_done"), sem("rope_done"), sem("rest_done")
        v_step = sem("v_step")
        part_done = sem("part_done")
        aug_in = [sem(f"aug_in{i}") for i in range(2)]
        max_in = [sem(f"max_in{i}") for i in range(2)]
        score_full, score_free = sem("score_full"), sem("score_free")
        st_full, exp_done, masked, p1_done = sem("st_full"), sem("exp_done"), sem("masked"), sem("p1_done")
        p2_dve, p2_pool = sem("p2_dve"), sem("p2_pool")
        pv_done, o_evac, o_scaled = sem("pv_done"), sem("o_evac"), sem("o_scaled")
        turn_hi = sem("turn_hi")
        stat_done, rstd_done, ln_done, yb_done = sem("stat_done"), sem("rstd_done"), sem("ln_done"), sem("yb_done")
        gate_act, gate_dve, hw_done = sem("gate_act"), sem("gate_dve"), sem("hw_done")
        dve_chain, pool_chain = sem("dve_chain"), sem("pool_chain")
        stored = [sem(f"stored{i}") for i in range(NT)]

        def tasks(j):
            todo = []
            if j % 4 == 0 and 0 < j <= UNITS:
                todo.append(("max", (j - 1) // G, (j // 4 - 1) % 2))
            for b in range(B):
                first = G * (b - 1)
                if b and j in (first + 2, first + 3, first + 4):
                    todo.append(("qkv", b, j - first - 2))
                if b and j == first + 5:
                    todo.append(("split", b, 0))
                t0 = G * b + 16
                todo += {
                    t0: [("attnT", b, 0), ("attnT", b, 1)],
                    t0 + 1: [("wo", b, 0)],
                    t0 + 2: [("norm1", b, 0), ("wo", b, 1)],
                    t0 + 3: [("norm1", b, 1), ("yT", b, 0), ("yT", b, 1)],
                    t0 + 4: [("adapt", b, 0), ("adapt", b, 1)],
                    t0 + 5: [("gate", b, 0), ("hT", b, 0), ("hT", b, 1)],
                    t0 + 6: [("ffn", b, 0)],
                    t0 + 7: [("norm2", b, 0), ("ffn", b, 1), ("norm2", b, 1)],
                }.get(j, [])
            return todo

        prologue = [("qkv", 0, 0), ("qkv", 0, 1), ("qkv", 0, 2), ("split", 0, 0)]
        order = prologue + [t for j in range(STEPS + 8) for t in tasks(j)]

        def nth(task, kinds):
            return sum(t[0] in kinds for t in order[:order.index(task)])

        ACC, TURN = ("qkv", "wo", "adapt", "ffn"), ("max", "attnT", "yT", "hT")

        chunks = [(wqkv[:, k, :], QKV, wq_hi[:, k, :], wq_lo[:, k, :], 1.0) for k in range(KC)]
        chunks += [(wo[:, k, :], D, wo_hi[:, k, :], wo_lo[:, k, :], 1.0) for k in range(KC)]
        chunks += [(wb[:, k, :], D, wb_hi[:, k, :], wb_lo[:, k, :], 1.0) for k in range(KC)]
        chunks += [(ag, KC * AG, ag_hi[:, :, :].rearrange("p k n -> p (k n)"),
                    ag_lo[:, :, :].rearrange("p k n -> p (k n)"), 1.0)]
        chunks += [(bw, D, bw_hi[:, :], bw_lo[:, :], SCALING)]
        chunk_step = {n: 1 + (n - KC) for n in range(KC, len(chunks))}

        block = ctx.enter_context(nc.Block())

        @block.sync
        def _(sp):
            def load_chunk(n):
                if n >= 3:
                    sp.wait_ge(raw_lo, n - 2)
                sp.dma_start(raw[:, n % 3, 0:chunks[n][1]], chunks[n][0]).then_inc(raw_in[n % 3], 16)

            def load_xT(b):
                if b:
                    sp.wait_ge(xT_lo_done, b)
                sp.dma_start(xT_raw[:, :, :], xT[b]).then_inc(xT_in, 16)

            def fill_aug(b):
                i = b % 2
                if b >= 2:
                    sp.wait_ge(st_full, 2 * G * (b - 1))
                for n in range(3):
                    sp.wait_ge(part_done, 3 * b + n + 1)
                    for s in range(len(Q_PARTS)):
                        if Q_PARTS[s] == n:
                            sp.dma_start(q_aug[i][16 * s:16 * s + 16, :, :],
                                         part[n][:, 0:R, :]).then_inc(aug_in[i], 16)
                        if K_PARTS[s] == n:
                            sp.dma_start(k_aug[i][16 * s:16 * s + 16, :, :],
                                         part[n][:, R, :]).then_inc(aug_in[i], 16)

            def fill_max(b, half_):
                n = 2 * b + half_
                sp.wait_ge(turn_free, nth(("max", b, half_), TURN) + 1)
                for c in range(2):
                    for t in range(NT):
                        sp.dma_start(q_aug[b % 2][ROWS + c:ROWS + c + 1, 4 * R * half_:4 * R * (half_ + 1), t * P:(t + 1) * P],
                                     m_part[c][t * 4 * R:(t + 1) * 4 * R, :]).then_inc(max_in[n % 2], 16)

            load_xT(0)
            for n in range(3):
                load_chunk(n)
            sp.dma_start(tables[:, :, :], tab).then_inc(small_in, 16)
            sp.dma_start(b_row[:, :], bbase).then_inc(small_in, 16)
            sp.dma_start(b_thr[:, :], bthr).then_inc(small_in, 16)
            load_chunk(3)
            fill_aug(0)
            for j in range(STEPS + 8):
                for n in chunk_step:
                    if chunk_step[n] == j + 1:
                        load_chunk(n)
                for b in range(B):
                    if j == G * (b - 1) and b:
                        load_xT(b)
                    if j == G * b + 14:
                        if b:
                            sp.wait_ge(acc_free, nth(("wo", b - 1, 1), ACC) + 1)
                        sp.dma_start(x_tok[:, :, :], x[b]).then_inc(x_in, 16)
                for kind, b, t in tasks(j):
                    if kind == "split":
                        fill_aug(b)
                    if kind == "max":
                        fill_max(b, t)
                    if kind == "norm2":
                        sp.wait_ge(ln_done, 4 * b + 2 + t + 1)
                        sp.dma_start(out[b][:, t, :], s_buf[:, t, :]).then_inc(stored[t], 16)
            for t in range(NT):
                sp.wait_ge(stored[t], 16 * B)

        @block.tensor
        def _(pe):
            def take(task, kinds, full, free):
                n = nth(task, kinds)
                if n:
                    pe.wait_ge(free, n)

            def three(dst, a_hi, a_lo, b_hi, b_lo, first, last):
                pe.matmul(dst, a_hi, b_hi, start=first, stop=False)
                pe.matmul(dst, a_hi, b_lo, start=False, stop=False)
                return pe.matmul(dst, a_lo, b_hi, start=False, stop=last)

            def qkv(b, i):
                take(("qkv", b, i), ACC, acc_full, acc_free)
                pe.wait_ge(xT_hi_done, b + 1)
                pe.wait_ge(xT_lo_done, b + 1)
                for tile in ((2 * i, 2 * i + 1) if i < 2 else (R,)):
                    dst = acc[:, (tile % 2) * S:(tile % 2 + 1) * S] if i < 2 else acc[:, 0:S]
                    for k in range(KC):
                        if b == 0 and i == 0 and tile == 0:
                            pe.wait_ge(raw_hi, k + 1)
                            pe.wait_ge(raw_lo, k + 1)
                        c = slice(tile * P, (tile + 1) * P)
                        last = three(dst, wq_hi[:, k, c], wq_lo[:, k, c], xT_hi[:, k, :], xT_lo[:, k, :],
                                     k == 0, k == KC - 1)
                if i == 2:
                    for t in range(NT):
                        for k in range(KC):
                            c = slice(t * P, (t + 1) * P)
                            last = three(acc[:, S + t * P:S + (t + 1) * P], xT_hi[:, k, c], xT_lo[:, k, c],
                                         wq_hi[:, k, QK:QKV], wq_lo[:, k, QK:QKV], k == 0, k == KC - 1)
                last.then_inc(acc_full, 1)

            def scores(u):
                b, g = divmod(u, G)
                if g == 0:
                    pe.wait_ge(aug_in[b % 2], 16 * 12 * (b // 2 + 1))
                    if b == 0:
                        pe.wait_ge(consts, 3)
                q, k = q_aug[b % 2], k_aug[b % 2]
                for n, (t, heads) in enumerate(((0, (0, 1, 2, 3)), (1, (0, 1)), (1, (2, 3)))):
                    use = 3 * u + n
                    if use >= 2:
                        pe.wait_ge(score_free, use - 1)
                    width = (t + 1) * P
                    for i, r in enumerate(heads):
                        pe.matmul(score[use % 2][:, i * width:(i + 1) * width],
                                  q[0:ROWS, R * g + r, t * P:(t + 1) * P], k[0:ROWS, g, 0:width],
                                  start=True, stop=False)
                        last = pe.matmul(score[use % 2][:, (i + 1) * width - P:(i + 1) * width],
                                         ident_b[:, :], mask_b[:, :], start=False, stop=True)
                    last.then_inc(score_full, 1)

            def scores_t(u):
                b, g = divmod(u, G)
                if g % 4 == 0:
                    n = 2 * b + g // 4
                    pe.wait_ge(max_in[n % 2], 64 * (n // 2 + 1))
                if u == 0:
                    pe.wait_ge(ones, 2)
                if u:
                    pe.wait_ge(exp_done, 2 * u - 1)
                q, k = q_aug[b % 2], k_aug[b % 2]
                for i in range(2):
                    last = pe.matmul(st_a[:, i * 512:(i + 1) * 512], k[:, g, 0:P],
                                     q[:, R * g + 2 * i:R * g + 2 * i + 2, :], start=True, stop=True)
                last.then_inc(st_full, 1)
                if u:
                    pe.wait_ge(exp_done, 2 * u)
                pe.matmul(st_b[:, :], k[:, g, P:S], q[:, R * g:R * g + R, P:S],
                          start=True, stop=True).then_inc(st_full, 1)

            def values(u):
                b, g = divmod(u, G)
                i = u % 2
                pe.wait_ge(p1_done, u + 1)
                pe.wait_ge(p2_dve, u + 1)
                pe.wait_ge(p2_pool, u + 1)
                if g == 0:
                    pe.wait_ge(v_step, 4 * (b + 1))
                if u == 0:
                    pe.wait_ge(ones, 3)
                if u:
                    pe.wait_ge(o_evac, 2 * u)
                v = [v_aug[:, b % V_RING, t, g, :] for t in range(NT)]
                for t in range(NT):
                    for r in range(R):
                        dst = o_view[:, R * t + r, :]
                        at = [(r * S + t * P, 0)] + ([(R * S + r * P, 1)] if t else [])
                        for c, kb in at:
                            for pp in (p1, p2):
                                last = pe.matmul(dst, pp[:, i, c:c + P], v[kb], start=(kb == 0 and pp is p1),
                                                 stop=((c, kb) == at[-1] and pp is p2))
                last.then_inc(pv_done, 1)

            def max_turn(b, half_):
                take(("max", b, half_), TURN, turn_full, turn_free)
                pe.wait_ge(score_free, 3 * 4 * (2 * b + half_ + 1))
                pe.transpose(turn[0:NT * 4 * R, 0:P], neg_max[:, half_, :, :].rearrange("p t h -> p (t h)"),
                             ident[:, :]).then_inc(turn_full, 1)

            def turn_rows(task, src, ready, count):
                take(task, TURN, turn_full, turn_free)
                pe.wait_ge(ready, count)
                for k in range(KC):
                    last = pe.transpose(turn[:, k * P:(k + 1) * P], src[:, k * P:(k + 1) * P], ident[:, :])
                last.then_inc(turn_full, 1)

            def dense(task, hi, lo, extra=False):
                _, b, t = task
                take(task, ACC, acc_full, acc_free)
                pe.wait_ge(turn_free, nth(("attnT" if task[0] == "wo" else "yT", b, t), TURN) + 1)
                if b == 0 and t == 0:
                    pe.wait_ge(raw_lo, {"wo": 8, "adapt": 13, "ffn": 14}[task[0]])
                    pe.wait_ge(raw_hi, {"wo": 8, "adapt": 13, "ffn": 14}[task[0]])
                n = hi.shape[2]
                for k in range(KC):
                    last = three(acc[:, 0:n], aT_hi[:, t, k, :], aT_lo[:, t, k, :], hi[:, k, :], lo[:, k, :],
                                 k == 0, k == KC - 1 and not extra)
                if extra:
                    pe.wait_ge(turn_free, nth(("hT", b, t), TURN) + 1)
                    last = three(acc[:, :], hT_hi[:, t, :], hT_lo[:, t, :], bw_hi[:, :], bw_lo[:, :], False, True)
                last.then_inc(acc_full, 1)

            for i in range(3):
                qkv(0, i)
            for j in range(STEPS + 8):
                if j < UNITS:
                    scores(j)
                if 0 <= j - LAG_ST < UNITS:
                    scores_t(j - LAG_ST)
                for task in tasks(j):
                    kind, b, t = task
                    if kind == "qkv":
                        qkv(b, t)
                    if kind == "max":
                        max_turn(b, t)
                    if kind == "attnT":
                        turn_rows(task, attn[:, t, :], o_scaled, G * (b + 1))
                    if kind == "yT":
                        turn_rows(task, y_buf[:, t, :], ln_done, 4 * b + t + 1)
                    if kind == "hT":
                        take(task, TURN, turn_full, turn_free)
                        pe.wait_ge(hw_done, b + 1)
                        pe.transpose(turn[:, 0:P], h_w[:, t, :], ident[:, :]).then_inc(turn_full, 1)
                    if kind == "wo":
                        dense(task, wo_hi, wo_lo)
                    if kind == "adapt":
                        dense(task, ag_hi, ag_lo)
                    if kind == "ffn":
                        dense(task, wb_hi, wb_lo, extra=True)
                if 0 <= j - LAG_PV < UNITS:
                    values(j - LAG_PV)

        @block.scalar
        def _(act):
            def high(n):
                act.wait_ge(raw_in[n % 3], 16 * (n // 3 + 1))
                _, cols, hi, _, scale = chunks[n]
                act.activation(hi, raw[:, n % 3, 0:cols], ACT.Copy, scale=scale).then_inc(raw_hi, 1)

            def x_high(b):
                act.wait_ge(xT_in, 16 * (b + 1))
                if b:
                    act.wait_ge(acc_full, nth(("qkv", b - 1, 2), ACC) + 1)
                act.activation(xT_hi[:, :, :], xT_raw[:, :, :], ACT.Copy).then_inc(xT_hi_done, 1)

            def qkv(b, i):
                act.wait_ge(acc_full, nth(("qkv", b, i), ACC) + 1)
                n = 3 * b + i
                if n:
                    act.wait_ge(rope_done, n)
                w = 2 * S if i < 2 else S
                act.activation(swapped[0:64, 0:w], acc[64:128, 0:w], ACT.Copy).then_inc(swap_done, 1)
                act.activation(swapped[64:128, 0:w], acc[0:64, 0:w], ACT.Copy).then_inc(swap_done, 1)
                if i == 2:
                    if b >= V_RING:
                        act.wait_ge(pv_done, G * (b - V_RING + 1))
                    v = v_aug[:, b % V_RING, :, :, :]
                    src = acc[:, S:2 * S].rearrange("p (t g d) -> p t g d", t=NT, g=G)
                    act.activation(v[:, :, :, 0:DH], src, ACT.Copy).then_inc(v_step, 1)
                    act.wait_ge(v_step, 4 * b + 2)
                    act.activation(v[:, :, :, DH:2 * DH], v_rest[:, :, :, :], ACT.Copy).then_inc(v_step, 1)

            def exps(u):
                i = u % 2
                if u >= 2:
                    act.wait_ge(p2_dve, u - 1)
                    act.wait_ge(p2_pool, u - 1)
                act.wait_ge(st_full, 2 * u + 1)
                act.activation(prob[:, i, 0:R * S], st_a[:, :], ACT.Exp, scale=SCALE).then_inc(exp_done, 1)
                act.wait_ge(st_full, 2 * u + 2)
                act.activation(prob[:, i, R * S:PCOLS], st_b[:, :], ACT.Exp, scale=SCALE).then_inc(exp_done, 1)

            def first_part(u):
                i = u % 2
                act.wait_ge(masked, 2 * u + 2)
                if u >= 2:
                    act.wait_ge(pv_done, u - 1)
                act.activation(p1[:, i, :], prob[:, i, :], ACT.Copy).then_inc(p1_done, 1)

            def turned(task):
                kind, b, t = task
                act.wait_ge(turn_full, nth(task, TURN) + 1)
                if kind == "attnT" and b:
                    act.wait_ge(acc_full, nth(("ffn", b - 1, t), ACC) + 1)
                if kind == "yT":
                    act.wait_ge(acc_full, nth(("wo", b, t), ACC) + 1)
                act.activation(aT_hi[:, t, :, :].rearrange("p k q -> p (k q)"), turn[:, :], ACT.Copy).then_inc(turn_hi, 1)

            def h_turned(task):
                kind, b, t = task
                act.wait_ge(turn_full, nth(task, TURN) + 1)
                if b:
                    act.wait_ge(acc_full, nth(("ffn", b - 1, t), ACC) + 1)
                act.activation(hT_hi[:, t, :], turn[:, 0:P], ACT.Copy).then_inc(turn_hi, 1)

            def adapt(task):
                kind, b, t = task
                act.wait_ge(acc_full, nth(task, ACC) + 1)
                if b:
                    act.wait_ge(hw_done, b)
                act.activation(h_raw[:, t, :], acc[:, 0:AG], ACT.Copy).then_inc(acc_free, 1)

            def gate(b):
                act.wait_ge(gate_dve, b + 1)
                if b == 0:
                    act.wait_ge(consts, 4)
                for t in range(NT):
                    act.activation(gate_e[:, t, :], h_raw[:, t, E * LR:E * LR + E], ACT.Exp, bias=neg_top[:, t:t + 1],
                                   accum_out=gate_c[:, 0, t:t + 1]).then_inc(gate_act, 1)
                act.activation(gate_c[:, 1, :], h_raw[:, :, AG - 2], ACT.Exp, scale=-1.0,
                               bias=b_thr[:, 0:1]).then_inc(gate_act, 1)

            def split_first(b):
                act.wait_ge(rope_done, 3 * (b + 1))
                if b:
                    act.wait_ge(aug_in[(b - 1) % 2], 16 * 12 * ((b - 1) // 2 + 1))
                act.activation(part[0][:, :, :], qk[:, :, :], ACT.Copy).then_inc(part_done, 1)

            def split_second(b):
                act.wait_ge(rest_done, b + 1)
                act.activation(part[1][:, :, :], qk[:, :, :], ACT.Copy).then_inc(part_done, 1)

            x_high(0)
            for n in range(KC):
                high(n)
            for i in range(3):
                qkv(0, i)
            split_first(0)
            split_second(0)
            for j in range(STEPS + 8):
                if 0 <= j - LAG_SPLIT < UNITS:
                    first_part(j - LAG_SPLIT)
                if 0 <= j - LAG_ST < UNITS:
                    exps(j - LAG_ST)
                for n in chunk_step:
                    if chunk_step[n] == j:
                        high(n)
                for b in range(1, B):
                    if j == G * (b - 1) + 1:
                        x_high(b)
                for task in tasks(j):
                    kind, b, t = task
                    if kind == "qkv":
                        qkv(b, t)
                    if kind == "split":
                        split_first(b)
                        split_second(b)
                    if kind in ("attnT", "yT"):
                        turned(task)
                    if kind == "hT":
                        h_turned(task)
                    if kind == "adapt":
                        adapt(task)
                    if kind == "gate":
                        gate(b)

        @block.vector
        def _(dve):
            links = [0]

            def link(ins):
                links[0] += 1
                ins.then_inc(dve_chain, 1)
                dve.wait_ge(dve_chain, links[0])

            def low(n):
                dve.wait_ge(raw_hi, n + 1)
                _, cols, hi, lo, scale = chunks[n]
                dve.scalar_tensor_tensor(lo, raw[:, n % 3, 0:cols], scale, hi.bitcast(F32), ALU.mult,
                                         ALU.subtract).then_inc(raw_lo, 1)

            def x_low(b):
                dve.wait_ge(xT_hi_done, b + 1)
                dve.tensor_tensor(xT_lo[:, :, :], xT_raw[:, :, :], xT_hi[:, :, :].bitcast(F32),
                                  ALU.subtract).then_inc(xT_lo_done, 1)

            def qkv(b, i):
                n = 3 * b + i
                dve.wait_ge(acc_full, nth(("qkv", b, i), ACC) + 1)
                if n == 0:
                    dve.wait_ge(small_in, 48)
                if n:
                    dve.wait_ge(rope_done, n)
                dve.wait_ge(swap_done, 2 * n + 2)
                if i == 2:
                    dve.wait_ge(v_step, 4 * b + 1)
                tiles = 2 if i < 2 else 1
                cos = tables[:, 0:1, :].broadcast_to([P, tiles, S])
                ins = dve.tensor_tensor(roped_cos[:, 0:tiles * S].rearrange("p (i t) -> p i t", i=tiles),
                                        acc[:, 0:tiles * S].rearrange("p (i t) -> p i t", i=tiles), cos, ALU.mult)
                if i == 2:
                    ins = dve.tensor_tensor(v_rest[:, :, :, :],
                                            acc[:, S:2 * S].rearrange("p (t g d) -> p t g d", t=NT, g=G),
                                            v_aug[:, b % V_RING, :, :, 0:DH], ALU.subtract)
                    ins.then_inc(v_step, 1)
                    dve.wait_ge(v_step, 4 * b + 2)
                    ins = dve.engine_nop()
                ins.then_inc(acc_free, 1)

            def maxima(u):
                b, g = divmod(u, G)
                n = u // 4
                if u % 4 == 0 and n >= 2:
                    dve.wait_ge(turn_full, nth(("max", (n - 2) // 2, n % 2), TURN) + 1)
                for i, (t, first, heads) in enumerate(((0, 0, 4), (1, 0, 2), (1, 2, 2))):
                    use = 3 * u + i
                    dve.wait_ge(score_full, use + 1)
                    at = R * (g % 4) + first
                    dve.tensor_reduce(neg_max[:, n % 2, t, at:at + heads],
                                      score[use % 2][:, :].rearrange("p (h k) -> p h k", h=heads), AX.X, ALU.max,
                                      negate=True).then_inc(score_free, 1)

            def max_parts(b, half_):
                n = 2 * b + half_
                dve.wait_ge(turn_full, nth(("max", b, half_), TURN) + 1)
                if n:
                    dve.wait_ge(max_in[(n - 1) % 2], 64 * ((n - 1) // 2 + 1))
                src = turn[0:NT * 4 * R, 0:P]
                link(dve.tensor_scalar(m_part[0][:, :], src, LIFT, None, ALU.add))
                dve.scalar_tensor_tensor(m_part[1][:, :], src, LIFT, m_part[0][:, :], ALU.add,
                                         ALU.subtract).then_inc(turn_free, 1)

            def second_part(u):
                i = u % 2
                dve.wait_ge(p1_done, u + 1)
                c = slice(0, R * S)
                dve.tensor_tensor(p2[:, i, c], prob[:, i, c], p1[:, i, c], ALU.subtract).then_inc(p2_dve, 1)

            def gather(u):
                i = u % 2
                dve.wait_ge(pv_done, u + 1)
                if u >= 2:
                    dve.wait_ge(o_scaled, u - 1)
                dve.tensor_reduce(o_sum[:, i, :, :], o_view[:, :, 0:3 * DH].rearrange("p n (c d) -> p n d c", c=3),
                                  AX.X, ALU.add).then_inc(o_evac, 1)
                dve.reciprocal(o_inv[:, i, :], o_view[:, :, 3 * DH]).then_inc(o_evac, 1)

            def turned(task):
                kind, b, t = task
                dve.wait_ge(turn_hi, nth(task, ("attnT", "yT", "hT")) + 1)
                if kind == "hT":
                    hi, lo, src = hT_hi[:, t, :], hT_lo[:, t, :], turn[:, 0:P]
                else:
                    hi, lo = (x_[:, t, :, :].rearrange("p k q -> p (k q)") for x_ in (aT_hi, aT_lo))
                    src = turn[:, :]
                dve.tensor_tensor(lo, src, hi.bitcast(F32), ALU.subtract).then_inc(turn_free, 1)

            def statistics(task):
                kind, b, t = task
                dve.wait_ge(acc_full, nth(task, ACC) + 1)
                if kind == "wo":
                    dve.wait_ge(x_in, 16 * (b + 1))
                    if b:
                        dve.wait_ge(stored[t], 16 * b)
                    res, dst = x_tok[:, t, :], s_buf[:, t, :]
                else:
                    dve.wait_ge(yb_done, NT * b + t + 1)
                    res, dst = s_buf[:, t, :], y_buf[:, t, :]
                dve.tensor_tensor(dst, acc[:, :], res, ALU.add).then_inc(acc_free, 1)
                dve.wait_ge(acc_free, nth(task, ACC) + 1)
                link(dve.bn_stats(stats[:, t, :], dst))
                dve.bn_aggr(mean_var[:, t, :], stats[:, t, :]).then_inc(stat_done, 1)

            def normalize(n, src, dst, t):
                dve.wait_ge(rstd_done, n + 1)
                dve.tensor_scalar(dst, src, mean_var[:, t, 0:1], rstd[:, t:t + 1], ALU.subtract,
                                  ALU.mult).then_inc(ln_done, 1)

            def gate(b):
                dve.wait_ge(acc_free, nth(("adapt", b, NT - 1), ACC) + 1)
                dve.tensor_reduce(neg_top[:, :], h_raw[:, :, E * LR:E * LR + E], AX.X, ALU.max,
                                  negate=True).then_inc(gate_dve, 1)
                dve.wait_ge(gate_act, 3 * (b + 1))
                link(dve.tensor_scalar(gate_c[:, 1, :], gate_c[:, 1, :], 1.0, None, ALU.add))
                link(dve.reciprocal(gate_r[:, :, :], gate_c[:, :, :]))
                wide = [P, NT, E]
                link(dve.tensor_scalar(gate_t[:, :], gate_r[:, 1, :], MAX_THRESHOLD, None, ALU.mult))
                link(dve.tensor_tensor(gate_w[:, :, :], gate_e[:, :, :],
                                       gate_r[:, 0, :].unsqueeze(2).broadcast_to(wide), ALU.mult))
                link(dve.tensor_tensor(gate_w[:, :, :], gate_w[:, :, :],
                                       gate_t[:, :].unsqueeze(2).broadcast_to(wide), ALU.subtract))
                link(dve.tensor_scalar(gate_w[:, :, :], gate_w[:, :, :], 0.0, None, ALU.max))
                link(dve.tensor_reduce(w_sum[:, :], gate_w[:, :, :], AX.X, ALU.add))
                link(dve.scalar_tensor_tensor(w_sum[:, :], w_sum[:, :], 0.0, w_sum[:, :], ALU.is_equal, ALU.add))
                link(dve.reciprocal(w_inv[:, :], w_sum[:, :]))
                link(dve.tensor_tensor(gate_w[:, :, :], gate_w[:, :, :],
                                       w_inv[:, :].unsqueeze(2).broadcast_to(wide), ALU.mult))
                if b:
                    dve.wait_ge(turn_full, nth(("hT", b - 1, NT - 1), TURN) + 1)
                for t in range(NT):
                    ins = dve.tensor_tensor(h_w[:, t, :].rearrange("p (e r) -> p e r", e=E),
                                            h_raw[:, t, 0:E * LR].rearrange("p (e r) -> p e r", e=E),
                                            gate_w[:, t, :].unsqueeze(2).broadcast_to([P, E, LR]), ALU.mult)
                ins.then_inc(hw_done, 1)

            for i in range(2):
                dve.memset(k_aug[i][ROWS:ROWS + 2, :, :], 1.0).then_inc(ones, 1)
            dve.memset(v_aug[:, :, :, :, 3 * DH:VC], 1.0).then_inc(ones, 1)
            x_low(0)
            for n in range(KC):
                low(n)
            for i in range(3):
                qkv(0, i)
            for j in range(STEPS + 8):
                if j < UNITS:
                    maxima(j)
                if 0 <= j - LAG_SPLIT < UNITS:
                    second_part(j - LAG_SPLIT)
                for n in chunk_step:
                    if chunk_step[n] == j:
                        low(n)
                for b in range(1, B):
                    if j == G * (b - 1) + 1:
                        x_low(b)
                for task in tasks(j):
                    kind, b, t = task
                    if kind == "qkv":
                        qkv(b, t)
                    if kind == "max":
                        max_parts(b, t)
                    if kind in ("attnT", "yT", "hT"):
                        turned(task)
                    if kind in ("wo", "ffn"):
                        statistics(task)
                    if kind == "norm1":
                        normalize(4 * b + t, s_buf[:, t, :], y_buf[:, t, :], t)
                    if kind == "norm2":
                        normalize(4 * b + 2 + t, y_buf[:, t, :], s_buf[:, t, :], t)
                    if kind == "gate":
                        gate(b)
                if 0 <= j - LAG_PV < UNITS:
                    gather(j - LAG_PV)

        @block.gpsimd
        def _(pool):
            links = [0]

            def link(ins):
                links[0] += 1
                ins.then_inc(pool_chain, 1)
                pool.wait_ge(pool_chain, links[0])

            link(pool.memset(ident[:, :], 1.0))
            link(pool.memset(mask_b[:, :], 0.0))
            link(pool.memset(ident_b[:, :], 1.0))
            diagonal = dict(compare_op=ALU.is_equal, fill=0.0, base=0, pattern=[[-1, P]], channel_multiplier=1)
            pool.affine_select(out=ident[:, :], in_=ident[:, :], **diagonal).then_inc(consts, 1)
            pool.affine_select(out=ident_b[:, :], in_=ident_b[:, :], **diagonal).then_inc(consts, 1)
            pool.affine_select(out=mask_b[:, :], in_=mask_b[:, :], compare_op=ALU.is_ge, fill=MASKED, base=0,
                               pattern=[[-1, P]], channel_multiplier=1).then_inc(consts, 1)
            pool.memset(half[:, :], -0.5)
            pool.wait_ge(small_in, 48)
            pool.tensor_scalar(b_thr[:, :], b_thr[:, :], -1.0, 0.0, ALU.mult, ALU.add).then_inc(consts, 1)

            def qkv(b, i):
                n = 3 * b + i
                tiles = 2 if i < 2 else 1
                w = tiles * S
                pool.wait_ge(swap_done, 2 * n + 2)
                sin = tables[:, 1:2, :].broadcast_to([P, tiles, S])
                swap = swapped[:, 0:w].rearrange("p (i t) -> p i t", i=tiles)
                link(pool.tensor_tensor(swap, swap, sin, ALU.mult))
                pool.wait_ge(acc_free, nth(("qkv", b, i), ACC) + 1)
                if b and i == 0:
                    pool.wait_ge(part_done, 3 * b)
                pool.tensor_tensor(qk[:, 2 * i:2 * i + tiles, :].rearrange("p i t -> p (i t)"), roped_cos[:, 0:w],
                                   swapped[:, 0:w], ALU.add).then_inc(rope_done, 1)
                if i == 2:
                    pool.wait_ge(v_step, 4 * b + 3)
                    pool.tensor_tensor(v_aug[:, b % V_RING, :, :, 2 * DH:3 * DH], v_rest[:, :, :, :],
                                       v_aug[:, b % V_RING, :, :, DH:2 * DH], ALU.subtract).then_inc(v_step, 1)

            def split(b):
                pool.wait_ge(part_done, 3 * b + 1)
                pool.tensor_tensor(qk[:, :, :], qk[:, :, :], part[0][:, :, :], ALU.subtract).then_inc(rest_done, 1)
                pool.wait_ge(part_done, 3 * b + 2)
                pool.wait_ge(rest_done, b + 1)
                pool.tensor_tensor(part[2][:, :, :], qk[:, :, :], part[1][:, :, :], ALU.subtract).then_inc(part_done, 1)

            def mask(u):
                i = u % 2
                for c, width in ((0, S), (R * S, P)):
                    pool.wait_ge(exp_done, 2 * u + (2 if c else 1))
                    v = prob[:, i, c:c + R * width].rearrange("p (r q) -> p r q", r=R)[:, :, 0:P]
                    pool.affine_select(out=v, in_=v, compare_op=ALU.is_ge, fill=0.0, base=0,
                                       pattern=[[0, R], [1, P]], channel_multiplier=-1).then_inc(masked, 1)

            def second_part(u):
                i = u % 2
                c = slice(R * S, PCOLS)
                pool.wait_ge(p1_done, u + 1)
                pool.tensor_tensor(p2[:, i, c], prob[:, i, c], p1[:, i, c], ALU.subtract).then_inc(p2_pool, 1)

            def scale(u):
                b, g = divmod(u, G)
                i = u % 2
                pool.wait_ge(o_evac, 2 * u + 2)
                if b and g == 0:
                    pool.wait_ge(turn_full, nth(("attnT", b - 1, NT - 1), TURN) + 1)
                dst = attn[:, :, g * R * DH:(g + 1) * R * DH].rearrange("p t (r d) -> p t r d", r=R)
                src = o_sum[:, i, :, :].rearrange("p (t r) d -> p t r d", t=NT)
                inv = o_inv[:, i, :].rearrange("p (t r) -> p t r", t=NT).unsqueeze(3).broadcast_to([P, NT, R, DH])
                pool.tensor_tensor(dst, src, inv, ALU.mult).then_inc(o_scaled, 1)

            def inverse_deviation(n, t):
                pool.wait_ge(stat_done, n + 1)
                link(pool.tensor_scalar(var_eps[:, t:t + 1], mean_var[:, t, 1:2], EPS, 0.0, ALU.add, ALU.add))
                pool.tensor_tensor(rstd[:, t:t + 1], var_eps[:, t:t + 1], half[:, t:t + 1],
                                   ALU.pow).then_inc(rstd_done, 1)

            for i in range(3):
                qkv(0, i)
            split(0)
            for j in range(STEPS + 8):
                if 0 <= j - LAG_SPLIT < UNITS:
                    second_part(j - LAG_SPLIT)
                if 0 <= j - LAG_ST < UNITS:
                    mask(j - LAG_ST)
                for task in tasks(j):
                    kind, b, t = task
                    if kind == "qkv":
                        qkv(b, t)
                    if kind == "split":
                        split(b)
                    if kind == "wo":
                        inverse_deviation(4 * b + t, t)
                    if kind == "ffn":
                        inverse_deviation(4 * b + 2 + t, t)
                    if kind == "norm1":
                        pool.wait_ge(ln_done, 4 * b + t + 1)
                        pool.tensor_tensor(s_buf[:, t, :], y_buf[:, t, :], b_row[:, :], ALU.add).then_inc(yb_done, 1)
                if 0 <= j - LAG_PV < UNITS:
                    scale(j - LAG_PV)


def kernel(L0_attn_x, L0_attn_w_qkv, L0_attn_w_o, L0_ffn_W_base, L0_ffn_b_base, L0_ffn_W_gate, L0_ffn_W_thr,
           L0_ffn_b_thr, L0_ffn_A_w, L0_ffn_B_w):
    import numpy as np
    import concourse.bacc as bacc
    from concourse.bass_utils import run_bass_kernel_spmd

    x = np.asarray(L0_attn_x)
    half_, freq, group = np.meshgrid(np.arange(2), np.arange(DH // 2), np.arange(G), indexing="ij")
    within = half_ * (DH // 2) + freq
    cols = [((R * group + r) * DH + within).ravel() for r in range(R)]
    cols += [(H * DH + group * DH + within).ravel(), np.arange(H * DH + G * DH, H * DH + 2 * G * DH)]
    cols = np.concatenate(cols)

    def chunked(w):
        return np.ascontiguousarray(w.T.reshape(KC, P, w.shape[0]).transpose(1, 0, 2))

    a_w = np.asarray(L0_ffn_A_w).reshape(E * LR, D)
    adapter = np.concatenate([a_w, np.asarray(L0_ffn_W_gate), np.asarray(L0_ffn_W_thr)[None],
                              np.zeros((1, D), np.float32)])
    inv_freq = (1.0 / 500000.0 ** (np.arange(0, DH, 2, dtype=np.float32) / np.float32(DH))).astype(np.float32)
    angle = np.outer(np.arange(S, dtype=np.float32), inv_freq).astype(np.float32)
    cos, sin = np.cos(angle), np.sin(angle)
    f = freq.ravel()
    sign = np.where(half_.ravel() == 0, -1.0, 1.0).astype(np.float32)
    tab = np.stack([cos[:, f].T, sin[:, f].T * sign[:, None]], axis=1).astype(np.float32)

    arrays = {
        "xT": np.ascontiguousarray(x.reshape(B, S, KC, P).transpose(0, 3, 2, 1)),
        "x": np.ascontiguousarray(x),
        "wqkv": chunked(np.asarray(L0_attn_w_qkv)[cols]),
        "wo": chunked(np.asarray(L0_attn_w_o)),
        "wb": chunked(np.asarray(L0_ffn_W_base)),
        "ag": chunked(adapter).reshape(P, KC * AG),
        "bw": np.ascontiguousarray(np.asarray(L0_ffn_B_w).transpose(0, 2, 1).reshape(E * LR, D)),
        "bbase": np.ascontiguousarray(np.broadcast_to(np.asarray(L0_ffn_b_base), (P, D))),
        "bthr": np.ascontiguousarray(np.broadcast_to(np.asarray(L0_ffn_b_thr), (P, 1))),
        "tab": np.ascontiguousarray(tab),
    }
    nc = bacc.Bacc("TRN2", target_bir_lowering=False, num_devices=1)
    aps = {n: nc.dram_tensor(f"in_{n}", a.shape, mybir.dt.from_np(a.dtype), kind="ExternalInput").ap()
           for n, a in arrays.items()}
    out = nc.dram_tensor("out", (B, S, D), F32, kind="ExternalOutput").ap()
    by_row = "b (t p) d -> b p t d"
    build(nc, aps["xT"], aps["x"].rearrange(by_row, p=P), aps["wqkv"], aps["wo"], aps["wb"], aps["ag"], aps["bw"],
          aps["bbase"], aps["bthr"], aps["tab"], out.rearrange(by_row, p=P))
    r = run_bass_kernel_spmd(nc, [{f"in_{n}": a for n, a in arrays.items()}], core_ids=[0])
    return r.results[0]["out"]
```

```python
from contextlib import ExitStack
import math

import concourse.bass as bass
from concourse import mybir

F32 = mybir.dt.float32
F32R = mybir.dt.float32r
BF16 = mybir.dt.bfloat16
F16 = mybir.dt.float16
ALU = mybir.AluOpType
ACT = mybir.ActivationFunctionType
AX = mybir.AxisListType

P = 128
B, S, D = 4, 256, 512
NT = S // P
KC = D // P
G, R, DH = 8, 4, 16
H = G * R
QK = (R + 1) * P
QKV = QK + G * DH
E, LR = 8, 16
AG = E * LR + E + 2
EPS = 1e-5
SCALING = 2.0
MAX_THRESHOLD = 0.125
SCALE = 1.0 / math.sqrt(DH)
LIFT = math.log(1024.0) / SCALE
Q_PARTS = (0, 1, 0, 1, 2, 0)
K_PARTS = (0, 0, 1, 1, 0, 2)
ROWS = 16 * len(Q_PARTS)
VC = 3 * DH + 1
UNITS = B * G
PCOLS = R * S + R * P
MASKED = -1e37
V_RING = 3

LAG_ST, LAG_SPLIT, LAG_PV, LAG_GATHER = 6, 7, 8, 8
STEPS = UNITS + 2 * G + 2


def build(nc, xT, x, wqkv, wo, wb, ag, bw, bbase, bthr, tab, out):
    ctx = ExitStack()
    with ctx:
        def sb(name, shape, dt):
            return ctx.enter_context(nc.sbuf_tensor(name, shape, dt))

        def sem(name):
            return ctx.enter_context(nc.semaphore(name))

        raw = sb("raw", [P, 3, QKV], F32)
        wq_hi, wq_lo = (sb(n, [P, KC, QKV], F32R) for n in ("wq_hi", "wq_lo"))
        wo_hi, wo_lo = (sb(n, [P, KC, D], F32R) for n in ("wo_hi", "wo_lo"))
        wb_hi, wb_lo = (sb(n, [P, KC, D], F32R) for n in ("wb_hi", "wb_lo"))
        ag_hi, ag_lo = (sb(n, [P, KC, AG], F32R) for n in ("ag_hi", "ag_lo"))
        bw_hi, bw_lo = (sb(n, [P, D], F32R) for n in ("bw_hi", "bw_lo"))
        xT_raw = sb("xT_raw", [P, KC, S], F32)
        xT_hi, xT_lo = (sb(n, [P, KC, S], F32R) for n in ("xT_hi", "xT_lo"))
        x_tok = sb("x_tok", [P, NT, D], F32)
        swapped = sb("swapped", [P, 2 * S], F32)
        roped_cos = sb("roped_cos", [P, 2 * S], F32)
        qk = sb("qk", [P, R + 1, S], F32)
        part = [sb(f"part{i}", [P, R + 1, S], BF16) for i in range(3)]
        q_aug = [sb(f"q_aug{i}", [ROWS + 2, H, S], BF16) for i in range(2)]
        k_aug = [sb(f"k_aug{i}", [ROWS + 2, G, S], BF16) for i in range(2)]
        v_aug = sb("v_aug", [P, V_RING, NT, G, VC], BF16)
        v_rest = sb("v_rest", [P, NT, G, DH], F32)
        neg_max = sb("neg_max", [P, 2, NT, 4 * R], F32)
        m_part = [sb(f"m_part{i}", [NT * 4 * R, P], BF16) for i in range(2)]
        prob = sb("prob", [P, 2, PCOLS], F32)
        p1 = sb("p1", [P, 2, PCOLS], F16)
        p2 = sb("p2", [P, 2, PCOLS], F16)
        o_sum = sb("o_sum", [P, 2, NT * R, DH], F32)
        o_inv = sb("o_inv", [P, 2, NT * R], F32)
        attn = sb("attn", [P, NT, D], F32)
        aT_hi, aT_lo = (sb(n, [P, NT, KC, P], F32R) for n in ("aT_hi", "aT_lo"))
        s_buf = sb("s_buf", [P, NT, D], F32)
        y_buf = sb("y_buf", [P, NT, D], F32)
        stats = sb("stats", [P, NT, 6], F32)
        mean_var = sb("mean_var", [P, NT, 2], F32)
        var_eps = sb("var_eps", [P, NT], F32)
        rstd = sb("rstd", [P, NT], F32)
        shift = sb("shift", [P, NT], F32)
        h_raw = sb("h_raw", [P, NT, AG], F32)
        neg_top = sb("neg_top", [P, NT], F32)
        gate_e = sb("gate_e", [P, NT, E], F32)
        gate_c = sb("gate_c", [P, 2, NT], F32)
        gate_r = sb("gate_r", [P, 2, NT], F32)
        gate_t = sb("gate_t", [P, NT], F32)
        gate_w = sb("gate_w", [P, NT, E], F32)
        w_sum = sb("w_sum", [P, NT], F32)
        w_inv = sb("w_inv", [P, NT], F32)
        h_w = sb("h_w", [P, NT, E * LR], F32)
        hT_hi, hT_lo = (sb(n, [P, NT, P], F32R) for n in ("hT_hi", "hT_lo"))
        ident = sb("ident", [P, P], F32)
        ident_b = sb("ident_b", [P, P], BF16)
        mask_b = sb("mask_b", [P, P], BF16)
        b_row = sb("b_row", [P, D], F32)
        b_thr = sb("b_thr", [P, 1], F32)
        tables = sb("tables", [P, 2, S], F32)
        half = sb("half", [P, NT], F32)

        score = [ctx.enter_context(nc.psum_tensor(f"score{i}", [P, 512], F32)) for i in range(2)]
        st_a = ctx.enter_context(nc.psum_tensor("st_a", [P, 1024], F32))
        st_b = ctx.enter_context(nc.psum_tensor("st_b", [P, 512], F32))
        o_ps = ctx.enter_context(nc.psum_tensor("o_ps", [P, 512], F32))
        acc = ctx.enter_context(nc.psum_tensor("acc", [P, 512], F32))
        turn_ps = ctx.enter_context(nc.psum_tensor("turn", [P, 512], F32))
        o_view = o_ps[:, 0:NT * R * VC].rearrange("p (n c) -> p n c", c=VC)

        raw_in = [sem(f"raw_in{i}") for i in range(3)]
        raw_hi = sem("raw_hi")
        raw_lo = sem("raw_lo")
        xT_in, x_in, small_in = sem("xT_in"), sem("x_in"), sem("small_in")
        xT_hi_done, xT_lo_done = sem("xT_hi_done"), sem("xT_lo_done")
        consts, ones = sem("consts"), sem("ones")
        acc_full, acc_free = sem("acc_full"), sem("acc_free")
        turn_full, turn_free = sem("turn_full"), sem("turn_free")
        swap_done, rope_done, rest_done = sem("swap_done"), sem("rope_done"), sem("rest_done")
        v_step = sem("v_step")
        part_done = sem("part_done")
        aug_in = [sem(f"aug_in{i}") for i in range(2)]
        max_in = [sem(f"max_in{i}") for i in range(2)]
        score_full, score_free = sem("score_full"), sem("score_free")
        st_full, exp_done, masked, p1_done = sem("st_full"), sem("exp_done"), sem("masked"), sem("p1_done")
        p2_dve, p2_pool = sem("p2_dve"), sem("p2_pool")
        pv_done, o_evac, o_scaled = sem("pv_done"), sem("o_evac"), sem("o_scaled")
        turn_hi = sem("turn_hi")
        stat_done, rstd_done, ln_done, yb_done = sem("stat_done"), sem("rstd_done"), sem("ln_done"), sem("yb_done")
        gate_act, gate_dve, hw_done = sem("gate_act"), sem("gate_dve"), sem("hw_done")
        dve_chain, pool_chain = sem("dve_chain"), sem("pool_chain")
        stored = [sem(f"stored{i}") for i in range(NT)]

        ACC, TURN = ("qkv", "wo", "adapt", "ffn"), ("max", "attnT", "yT", "hT")

        def qkv_steps(b):
            return {1: (-1, 1, 2), 2: (5, 7, 9), 3: (14, 15, 16)}[b]

        def tasks(j):
            todo = []
            for b in range(B):
                if b and j in qkv_steps(b):
                    todo.append(("qkv", b, qkv_steps(b).index(j)))
                t0 = G * b + 16
                todo += {
                    t0: [("attnT", b, 0)],
                    t0 + 1: [("attnT", b, 1), ("wo", b, 0)],
                    t0 + 2: [("wo", b, 1)],
                    t0 + 3: [("yT", b, 0)],
                    t0 + 4: [("yT", b, 1)],
                    t0 + 5: [("adapt", b, 0)],
                    t0 + 7: [("hT", b, 0), ("hT", b, 1), ("ffn", b, 0)],
                    t0 + 8: [("ffn", b, 1)],
                }.get(j, [])
            if j % 4 == 0 and 0 < j <= UNITS:
                todo.insert(0, ("max", (j - 1) // G, (j // 4 - 1) % 2))
            return todo

        def turns(j, late):
            now = [t for t in tasks(j) if t[0] in TURN]
            return [t for t in now if (t[0] + str(t[2]) in ("attnT0", "yT1", "hT1")) == late]

        def dense_of(j):
            return [t for t in tasks(j) if t[0] in ACC]

        prologue = [("qkv", 0, i) for i in range(3)]
        order = prologue + [t for j in range(-1, STEPS) for t in dense_of(j)]
        order += [t for j in range(STEPS) for late in (False, True) for t in turns(j, late)]

        def nth(task, kinds):
            return sum(t[0] in kinds for t in order[:order.index(task)])

        chunks = [(wqkv[:, k, :], QKV, wq_hi[:, k, :], wq_lo[:, k, :], 1.0) for k in range(KC)]
        chunks += [(wo[:, k, :], D, wo_hi[:, k, :], wo_lo[:, k, :], 1.0) for k in range(KC)]
        chunks += [(wb[:, k, :], D, wb_hi[:, k, :], wb_lo[:, k, :], 1.0) for k in range(KC)]
        chunks += [(ag, KC * AG, ag_hi[:, :, :].rearrange("p k n -> p (k n)"),
                    ag_lo[:, :, :].rearrange("p k n -> p (k n)"), 1.0)]
        chunks += [(bw, D, bw_hi[:, :], bw_lo[:, :], SCALING)]
        chunk_step = {n: 1 + (n - KC) for n in range(KC, len(chunks))}

        block = ctx.enter_context(nc.Block())

        @block.sync
        def _(sp):
            def load_chunk(n):
                if n >= 3:
                    sp.wait_ge(raw_lo, n - 2)
                sp.dma_start(raw[:, n % 3, 0:chunks[n][1]], chunks[n][0]).then_inc(raw_in[n % 3], 16)

            def load_xT(b):
                if b:
                    sp.wait_ge(xT_lo_done, b)
                sp.dma_start(xT_raw[:, :, :], xT[b]).then_inc(xT_in, 16)

            def fill_aug(b):
                i = b % 2
                if b >= 2:
                    sp.wait_ge(st_full, 2 * G * (b - 1))
                sp.wait_ge(part_done, 9 * (b + 1))
                for s in range(len(Q_PARTS)):
                    sp.dma_start(q_aug[i][16 * s:16 * s + 16, :, :],
                                 part[Q_PARTS[s]][:, 0:R, :]).then_inc(aug_in[i], 16)
                    sp.dma_start(k_aug[i][16 * s:16 * s + 16, :, :],
                                 part[K_PARTS[s]][:, R, :]).then_inc(aug_in[i], 16)

            def fill_max(b, half_):
                n = 2 * b + half_
                sp.wait_ge(turn_free, nth(("max", b, half_), TURN) + 1)
                for c in range(2):
                    for t in range(NT):
                        sp.dma_start(q_aug[b % 2][ROWS + c:ROWS + c + 1, 4 * R * half_:4 * R * (half_ + 1), t * P:(t + 1) * P],
                                     m_part[c][t * 4 * R:(t + 1) * 4 * R, :]).then_inc(max_in[n % 2], 16)

            load_xT(0)
            for n in range(3):
                load_chunk(n)
            sp.dma_start(tables[:, :, :], tab).then_inc(small_in, 16)
            sp.dma_start(b_row[:, :], bbase).then_inc(small_in, 16)
            sp.dma_start(b_thr[:, :], bthr).then_inc(small_in, 16)
            load_chunk(3)
            load_xT(1)
            fill_aug(0)
            for j in range(STEPS):
                for n in chunk_step:
                    if chunk_step[n] == j + 1:
                        load_chunk(n)
                for b in range(B):
                    if b > 1 and j == max(qkv_steps(b)[0] - 4, 0):
                        load_xT(b)
                    if j == G * b + 14:
                        if b:
                            sp.wait_ge(acc_free, nth(("wo", b - 1, 1), ACC) + 1)
                        sp.dma_start(x_tok[:, :, :], x[b]).then_inc(x_in, 16)
                for kind, b, t in tasks(j):
                    if kind == "max":
                        fill_max(b, t)
                for b in range(1, B):
                    if j == (G * (b - 1) + 5 if b > 1 else qkv_steps(b)[2] + 2):
                        fill_aug(b)
                for kind, b, t in dense_of(j - 1):
                    if kind == "ffn":
                        sp.wait_ge(ln_done, 4 * b + 2 + t + 1)
                        sp.dma_start(out[b][:, t, :], s_buf[:, t, :]).then_inc(stored[t], 16)
            for t in range(NT):
                sp.wait_ge(stored[t], 16 * B)

        @block.tensor
        def _(pe):
            def take(task, kinds, full, free):
                n = nth(task, kinds)
                if n:
                    pe.wait_ge(free, n)

            def three(dst, a_hi, a_lo, b_hi, b_lo, first, last):
                pe.matmul(dst, a_hi, b_hi, start=first, stop=False)
                pe.matmul(dst, a_hi, b_lo, start=False, stop=False)
                return pe.matmul(dst, a_lo, b_hi, start=False, stop=last)

            def dense_quarter(task, q):
                kind, b, t = task
                if q == 0:
                    take(task, ACC, acc_full, acc_free)
                if kind == "qkv":
                    if q == 0 and t == 0:
                        pe.wait_ge(xT_hi_done, b + 1)
                        pe.wait_ge(xT_lo_done, b + 1)
                    if t < 2:
                        tile, ks, dst = 2 * t + q // 2, (2 * (q % 2), 2 * (q % 2) + 1), acc[:, (q // 2) * S:(q // 2 + 1) * S]
                    elif q < 2:
                        tile, ks, dst = R, (2 * q, 2 * q + 1), acc[:, 0:S]
                    if t < 2 or q < 2:
                        for k in ks:
                            if b == 0 and t == 0 and q < 2:
                                pe.wait_ge(raw_hi, k + 1)
                                pe.wait_ge(raw_lo, k + 1)
                            c = slice(tile * P, (tile + 1) * P)
                            last = three(dst, wq_hi[:, k, c], wq_lo[:, k, c], xT_hi[:, k, :], xT_lo[:, k, :],
                                         k == 0, k == KC - 1)
                    else:
                        for k in range(KC):
                            c = slice((q - 2) * P, (q - 1) * P)
                            last = three(acc[:, S + (q - 2) * P:S + (q - 1) * P], xT_hi[:, k, c], xT_lo[:, k, c],
                                         wq_hi[:, k, QK:QKV], wq_lo[:, k, QK:QKV], k == 0, k == KC - 1)
                elif kind == "adapt":
                    tt = q // 2
                    pe.wait_ge(turn_free, nth(("yT", b, tt), TURN) + 1)
                    for k in (2 * (q % 2), 2 * (q % 2) + 1):
                        if b == 0 and q == 0:
                            pe.wait_ge(raw_lo, 3 * KC + 1)
                        last = three(acc[:, tt * S:tt * S + AG], aT_hi[:, tt, k, :], aT_lo[:, tt, k, :],
                                     ag_hi[:, k, :], ag_lo[:, k, :], k == 0, k == KC - 1)
                else:
                    if q == 0:
                        pe.wait_ge(turn_free, nth(("attnT" if kind == "wo" else "yT", b, t), TURN) + 1)
                        if b == 0 and t == 0:
                            pe.wait_ge(raw_lo, 2 * KC if kind == "wo" else 3 * KC + 2)
                    hi, lo = (wo_hi, wo_lo) if kind == "wo" else (wb_hi, wb_lo)
                    last = three(acc[:, :], aT_hi[:, t, q, :], aT_lo[:, t, q, :], hi[:, q, :], lo[:, q, :],
                                 q == 0, q == KC - 1 and kind == "wo")
                    if kind == "ffn" and q == KC - 1:
                        pe.wait_ge(turn_free, nth(("hT", b, t), TURN) + 1)
                        last = three(acc[:, :], hT_hi[:, t, :], hT_lo[:, t, :], bw_hi[:, :], bw_lo[:, :], False, True)
                if q == 3:
                    last.then_inc(acc_full, 1)

            def scores(u, n):
                b, g = divmod(u, G)
                if g == 0 and n == 0:
                    pe.wait_ge(aug_in[b % 2], 16 * 12 * (b // 2 + 1))
                    if b == 0:
                        pe.wait_ge(consts, 3)
                q, k = q_aug[b % 2], k_aug[b % 2]
                t, heads = ((0, (0, 1, 2, 3)), (1, (0, 1)), (1, (2, 3)))[n]
                use = 3 * u + n
                if use >= 2:
                    pe.wait_ge(score_free, use - 1)
                width = (t + 1) * P
                for i, r in enumerate(heads):
                    pe.matmul(score[use % 2][:, i * width:(i + 1) * width],
                              q[0:ROWS, R * g + r, t * P:(t + 1) * P], k[0:ROWS, g, 0:width],
                              start=True, stop=False)
                    last = pe.matmul(score[use % 2][:, (i + 1) * width - P:(i + 1) * width],
                                     ident_b[:, :], mask_b[:, :], start=False, stop=True)
                last.then_inc(score_full, 1)

            def scores_t(u, late):
                b, g = divmod(u, G)
                if g % 4 == 0 and not late:
                    n = 2 * b + g // 4
                    pe.wait_ge(max_in[n % 2], 64 * (n // 2 + 1))
                if u == 0:
                    pe.wait_ge(ones, 2)
                if u:
                    pe.wait_ge(exp_done, 2 * u if late else 2 * u - 1)
                q, k = q_aug[b % 2], k_aug[b % 2]
                if late:
                    last = pe.matmul(st_b[:, :], k[:, g, P:S], q[:, R * g:R * g + R, P:S], start=True, stop=True)
                else:
                    for i in range(2):
                        last = pe.matmul(st_a[:, i * 512:(i + 1) * 512], k[:, g, 0:P],
                                         q[:, R * g + 2 * i:R * g + 2 * i + 2, :], start=True, stop=True)
                last.then_inc(st_full, 1)

            def values(u):
                b, g = divmod(u, G)
                i = u % 2
                pe.wait_ge(p1_done, u + 1)
                pe.wait_ge(p2_dve, u + 1)
                pe.wait_ge(p2_pool, u + 1)
                if g == 0:
                    pe.wait_ge(v_step, 3 * (b + 1))
                if u == 0:
                    pe.wait_ge(ones, 3)
                if u:
                    pe.wait_ge(o_evac, 2 * u)
                v = [v_aug[:, b % V_RING, t, g, :] for t in range(NT)]
                for t in range(NT):
                    for r in range(R):
                        dst = o_view[:, R * t + r, :]
                        at = [(r * S + t * P, 0)] + ([(R * S + r * P, 1)] if t else [])
                        for c, kb in at:
                            for pp in (p1, p2):
                                last = pe.matmul(dst, pp[:, i, c:c + P], v[kb], start=(kb == 0 and pp is p1),
                                                 stop=((c, kb) == at[-1] and pp is p2))
                last.then_inc(pv_done, 1)

            def max_turn(b, half_):
                take(("max", b, half_), TURN, turn_full, turn_free)
                pe.wait_ge(score_free, 3 * 4 * (2 * b + half_ + 1))
                pe.transpose(turn_ps[0:NT * 4 * R, 0:P], neg_max[:, half_, :, :].rearrange("p t h -> p (t h)"),
                             ident[:, :]).then_inc(turn_full, 1)

            def turn_rows(task, src, ready, count):
                take(task, TURN, turn_full, turn_free)
                pe.wait_ge(ready, count)
                for k in range(KC):
                    last = pe.transpose(turn_ps[:, k * P:(k + 1) * P], src[:, k * P:(k + 1) * P], ident[:, :])
                last.then_inc(turn_full, 1)

            def turn(task):
                kind, b, t = task
                if kind == "max":
                    max_turn(b, t)
                if kind == "attnT":
                    turn_rows(task, attn[:, t, :], o_scaled, G * (b + 1))
                if kind == "yT":
                    turn_rows(task, y_buf[:, t, :], ln_done, 4 * b + t + 1)
                if kind == "hT":
                    take(task, TURN, turn_full, turn_free)
                    pe.wait_ge(hw_done, b + 1)
                    pe.transpose(turn_ps[:, 0:P], h_w[:, t, :], ident[:, :]).then_inc(turn_full, 1)

            def dense(j, q):
                for task in tasks(j):
                    if task[0] in ACC:
                        dense_quarter(task, q)

            for i in range(3):
                for q in range(4):
                    dense_quarter(("qkv", 0, i), q)
            for q in range(4):
                dense(-1, q)
            for j in range(STEPS):
                first, second, third = j < UNITS, 0 <= j - LAG_ST < UNITS, 0 <= j - LAG_PV < UNITS
                if second:
                    scores_t(j - LAG_ST, False)
                    scores_t(j - LAG_ST, True)
                if first:
                    scores(j, 0)
                if first:
                    scores(j, 1)
                if third:
                    values(j - LAG_PV)
                for task in turns(j, False):
                    turn(task)
                dense(j, 0)
                dense(j, 1)
                if first:
                    scores(j, 2)
                dense(j, 2)
                dense(j, 3)
                for task in turns(j, True):
                    turn(task)

        @block.scalar
        def _(act):
            def high(n):
                act.wait_ge(raw_in[n % 3], 16 * (n // 3 + 1))
                _, cols, hi, _, scale = chunks[n]
                act.activation(hi, raw[:, n % 3, 0:cols], ACT.Copy, scale=scale).then_inc(raw_hi, 1)

            def x_high(b):
                act.wait_ge(xT_in, 16 * (b + 1))
                if b:
                    act.wait_ge(acc_full, nth(("qkv", b - 1, 2), ACC) + 1)
                act.activation(xT_hi[:, :, :], xT_raw[:, :, :], ACT.Copy).then_inc(xT_hi_done, 1)

            def qkv(b, i):
                act.wait_ge(acc_full, nth(("qkv", b, i), ACC) + 1)
                n = 3 * b + i
                if n:
                    act.wait_ge(rope_done, n)
                w = 2 * S if i < 2 else S
                act.activation(swapped[0:64, 0:w], acc[64:128, 0:w], ACT.Copy).then_inc(swap_done, 1)
                act.activation(swapped[64:128, 0:w], acc[0:64, 0:w], ACT.Copy).then_inc(swap_done, 1)
                if i == 2:
                    if b >= V_RING:
                        act.wait_ge(pv_done, G * (b - V_RING + 1))
                    v = v_aug[:, b % V_RING, :, :, :]
                    src = acc[:, S:2 * S].rearrange("p (t g d) -> p t g d", t=NT, g=G)
                    act.activation(v[:, :, :, 0:DH], src, ACT.Copy).then_inc(v_step, 1)

            def v_second(b):
                act.wait_ge(acc_free, nth(("qkv", b, 2), ACC) + 1)
                act.activation(v_aug[:, b % V_RING, :, :, DH:2 * DH], v_rest[:, :, :, :], ACT.Copy).then_inc(v_step, 1)

            def exps(u, late):
                i = u % 2
                if not late:
                    if u >= 2:
                        act.wait_ge(p2_dve, u - 1)
                        act.wait_ge(p2_pool, u - 1)
                    act.wait_ge(st_full, 2 * u + 1)
                    act.activation(prob[:, i, 0:R * S], st_a[:, :], ACT.Exp, scale=SCALE).then_inc(exp_done, 1)
                else:
                    act.wait_ge(st_full, 2 * u + 2)
                    act.activation(prob[:, i, R * S:PCOLS], st_b[:, :], ACT.Exp, scale=SCALE).then_inc(exp_done, 1)

            def first_part(u):
                i = u % 2
                act.wait_ge(masked, 2 * u + 2)
                if u >= 2:
                    act.wait_ge(pv_done, u - 1)
                act.activation(p1[:, i, :], prob[:, i, :], ACT.Copy).then_inc(p1_done, 1)

            def turned(task):
                kind, b, t = task
                act.wait_ge(turn_full, nth(task, TURN) + 1)
                if kind == "attnT" and b:
                    act.wait_ge(acc_full, nth(("ffn", b - 1, t), ACC) + 1)
                if kind == "yT":
                    act.wait_ge(acc_full, nth(("wo", b, t), ACC) + 1)
                act.activation(aT_hi[:, t, :, :].rearrange("p k q -> p (k q)"), turn_ps[:, :], ACT.Copy).then_inc(turn_hi, 1)

            def h_turned(task):
                kind, b, t = task
                act.wait_ge(turn_full, nth(task, TURN) + 1)
                if b:
                    act.wait_ge(acc_full, nth(("ffn", b - 1, t), ACC) + 1)
                act.activation(hT_hi[:, t, :], turn_ps[:, 0:P], ACT.Copy).then_inc(turn_hi, 1)

            def adapt(task):
                kind, b, t = task
                act.wait_ge(acc_full, nth(task, ACC) + 1)
                if b:
                    act.wait_ge(hw_done, b)
                act.activation(h_raw[:, :, :], acc[:, :].rearrange("p (t n) -> p t n", t=NT)[:, :, 0:AG],
                               ACT.Copy).then_inc(acc_free, 1)

            def normalize(n, src, dst, t):
                act.wait_ge(rstd_done, n + 1)
                act.activation(dst, src, ACT.Identity, bias=shift[:, t:t + 1],
                               scale=rstd[:, t:t + 1]).then_inc(ln_done, 1)

            def turn(task):
                if task[0] in ("attnT", "yT"):
                    turned(task)
                if task[0] == "hT":
                    h_turned(task)

            def gate(b):
                act.wait_ge(gate_dve, b + 1)
                if b == 0:
                    act.wait_ge(consts, 4)
                for t in range(NT):
                    act.activation(gate_e[:, t, :], h_raw[:, t, E * LR:E * LR + E], ACT.Exp, bias=neg_top[:, t:t + 1],
                                   accum_out=gate_c[:, 0, t:t + 1]).then_inc(gate_act, 1)
                act.activation(gate_c[:, 1, :], h_raw[:, :, AG - 2], ACT.Exp, scale=-1.0,
                               bias=b_thr[:, 0:1]).then_inc(gate_act, 1)

            def tiles_of(i):
                return slice(2 * i, min(2 * i + 2, R + 1))

            def split_first(b, i):
                act.wait_ge(rope_done, 3 * b + i + 1)
                if b:
                    act.wait_ge(aug_in[(b - 1) % 2], 16 * 12 * ((b - 1) // 2 + 1))
                act.activation(part[0][:, tiles_of(i), :], qk[:, tiles_of(i), :], ACT.Copy).then_inc(part_done, 1)

            def split_second(b, i):
                act.wait_ge(rest_done, 3 * b + i + 1)
                act.activation(part[1][:, tiles_of(i), :], qk[:, tiles_of(i), :], ACT.Copy).then_inc(part_done, 1)

            x_high(0)
            for n in range(KC):
                high(n)
            for i in range(3):
                qkv(0, i)
                split_first(0, i)
                split_second(0, i)
            v_second(0)
            x_high(1)
            for j in range(STEPS):
                before = dense_of(j - 1)
                for task in turns(j - 1, True):
                    turn(task)
                if 0 <= j - LAG_SPLIT < UNITS:
                    first_part(j - LAG_SPLIT)
                for kind, b, t in before:
                    if kind == "qkv":
                        qkv(b, t)
                    if kind == "adapt":
                        adapt((kind, b, t))
                if 0 <= j - LAG_ST < UNITS:
                    exps(j - LAG_ST, False)
                if 0 <= j - LAG_ST < UNITS:
                    exps(j - LAG_ST, True)
                for task in turns(j, False):
                    turn(task)
                for kind, b, t in dense_of(j - 2):
                    if kind == "qkv":
                        split_first(b, t)
                for kind, b, t in before:
                    if kind == "wo":
                        normalize(4 * b + t, s_buf[:, t, :], y_buf[:, t, :], t)
                    if kind == "ffn":
                        normalize(4 * b + 2 + t, y_buf[:, t, :], s_buf[:, t, :], t)
                    if kind == "adapt":
                        gate(b)
                    if kind == "qkv" and t == 2:
                        v_second(b)
                for kind, b, t in dense_of(j - 2):
                    if kind == "qkv":
                        split_second(b, t)
                for n in chunk_step:
                    if chunk_step[n] == j:
                        high(n)
                for b in range(2, B):
                    if j == qkv_steps(b)[0] - 1:
                        x_high(b)

        @block.vector
        def _(dve):
            links = [0]

            def link(ins):
                links[0] += 1
                ins.then_inc(dve_chain, 1)
                dve.wait_ge(dve_chain, links[0])

            def low(n):
                dve.wait_ge(raw_hi, n + 1)
                _, cols, hi, lo, scale = chunks[n]
                dve.scalar_tensor_tensor(lo, raw[:, n % 3, 0:cols], scale, hi.bitcast(F32), ALU.mult,
                                         ALU.subtract).then_inc(raw_lo, 1)

            def x_low(b):
                dve.wait_ge(xT_hi_done, b + 1)
                dve.tensor_tensor(xT_lo[:, :, :], xT_raw[:, :, :], xT_hi[:, :, :].bitcast(F32),
                                  ALU.subtract).then_inc(xT_lo_done, 1)

            def qkv(b, i):
                n = 3 * b + i
                dve.wait_ge(acc_full, nth(("qkv", b, i), ACC) + 1)
                if n == 0:
                    dve.wait_ge(small_in, 48)
                if n:
                    dve.wait_ge(rope_done, n)
                dve.wait_ge(swap_done, 2 * n + 2)
                if i == 2:
                    dve.wait_ge(v_step, 3 * b + 1)
                tiles = 2 if i < 2 else 1
                cos = tables[:, 0:1, :].broadcast_to([P, tiles, S])
                ins = dve.tensor_tensor(roped_cos[:, 0:tiles * S].rearrange("p (i t) -> p i t", i=tiles),
                                        acc[:, 0:tiles * S].rearrange("p (i t) -> p i t", i=tiles), cos, ALU.mult)
                if i == 2:
                    ins = dve.tensor_tensor(v_rest[:, :, :, :],
                                            acc[:, S:2 * S].rearrange("p (t g d) -> p t g d", t=NT, g=G),
                                            v_aug[:, b % V_RING, :, :, 0:DH], ALU.subtract)
                ins.then_inc(acc_free, 1)

            def maximum(u, i):
                b, g = divmod(u, G)
                n = u // 4
                if u % 4 == 0 and i == 0 and n >= 2:
                    dve.wait_ge(turn_full, nth(("max", (n - 2) // 2, n % 2), TURN) + 1)
                t, first, heads = ((0, 0, 4), (1, 0, 2), (1, 2, 2))[i]
                use = 3 * u + i
                dve.wait_ge(score_full, use + 1)
                at = R * (g % 4) + first
                dve.tensor_reduce(neg_max[:, n % 2, t, at:at + heads],
                                  score[use % 2][:, :].rearrange("p (h k) -> p h k", h=heads), AX.X, ALU.max,
                                  negate=True).then_inc(score_free, 1)

            def max_parts(b, half_):
                n = 2 * b + half_
                dve.wait_ge(turn_full, nth(("max", b, half_), TURN) + 1)
                if n:
                    dve.wait_ge(max_in[(n - 1) % 2], 64 * ((n - 1) // 2 + 1))
                src = turn_ps[0:NT * 4 * R, 0:P]
                link(dve.tensor_scalar(m_part[0][:, :], src, LIFT, None, ALU.add))
                dve.scalar_tensor_tensor(m_part[1][:, :], src, LIFT, m_part[0][:, :], ALU.add,
                                         ALU.subtract).then_inc(turn_free, 1)

            def second_part(u):
                i = u % 2
                dve.wait_ge(p1_done, u + 1)
                c = slice(0, R * S)
                dve.tensor_tensor(p2[:, i, c], prob[:, i, c], p1[:, i, c], ALU.subtract).then_inc(p2_dve, 1)

            def gather(u):
                i = u % 2
                dve.wait_ge(pv_done, u + 1)
                if u >= 2:
                    dve.wait_ge(o_scaled, u - 1)
                dve.tensor_reduce(o_sum[:, i, :, :], o_view[:, :, 0:3 * DH].rearrange("p n (c d) -> p n d c", c=3),
                                  AX.X, ALU.add).then_inc(o_evac, 1)
                dve.reciprocal(o_inv[:, i, :], o_view[:, :, 3 * DH]).then_inc(o_evac, 1)

            def turned(task):
                kind, b, t = task
                dve.wait_ge(turn_hi, nth(task, ("attnT", "yT", "hT")) + 1)
                if kind == "hT":
                    hi, lo, src = hT_hi[:, t, :], hT_lo[:, t, :], turn_ps[:, 0:P]
                else:
                    hi, lo = (x_[:, t, :, :].rearrange("p k q -> p (k q)") for x_ in (aT_hi, aT_lo))
                    src = turn_ps[:, :]
                dve.tensor_tensor(lo, src, hi.bitcast(F32), ALU.subtract).then_inc(turn_free, 1)

            def statistics(task):
                kind, b, t = task
                dve.wait_ge(acc_full, nth(task, ACC) + 1)
                if kind == "wo":
                    dve.wait_ge(x_in, 16 * (b + 1))
                    if b:
                        dve.wait_ge(stored[t], 16 * b)
                    res, dst = x_tok[:, t, :], s_buf[:, t, :]
                else:
                    dve.wait_ge(yb_done, NT * b + t + 1)
                    res, dst = s_buf[:, t, :], y_buf[:, t, :]
                dve.tensor_tensor(dst, acc[:, :], res, ALU.add).then_inc(acc_free, 1)
                dve.wait_ge(acc_free, nth(task, ACC) + 1)
                link(dve.bn_stats(stats[:, t, :], dst))
                dve.bn_aggr(mean_var[:, t, :], stats[:, t, :]).then_inc(stat_done, 1)

            def chained(ins):
                links[0] += 1
                ins.then_inc(dve_chain, 1)

            def after_chained():
                dve.wait_ge(dve_chain, links[0])

            wide = [P, NT, E]

            def gate_top(b):
                dve.wait_ge(acc_free, nth(("adapt", b, 0), ACC) + 1)
                dve.tensor_reduce(neg_top[:, :], h_raw[:, :, E * LR:E * LR + E], AX.X, ALU.max,
                                  negate=True).then_inc(gate_dve, 1)

            def gate_one(b):
                dve.wait_ge(gate_act, 3 * (b + 1))
                chained(dve.tensor_scalar(gate_c[:, 1, :], gate_c[:, 1, :], 1.0, None, ALU.add))

            def gate_inverse(b):
                after_chained()
                link(dve.reciprocal(gate_r[:, :, :], gate_c[:, :, :]))
                dve.tensor_scalar(gate_t[:, :], gate_r[:, 1, :], MAX_THRESHOLD, None, ALU.mult)
                chained(dve.tensor_tensor(gate_w[:, :, :], gate_e[:, :, :],
                                          gate_r[:, 0, :].unsqueeze(2).broadcast_to(wide), ALU.mult))

            def gate_threshold(b):
                after_chained()
                link(dve.tensor_tensor(gate_w[:, :, :], gate_w[:, :, :],
                                       gate_t[:, :].unsqueeze(2).broadcast_to(wide), ALU.subtract))
                chained(dve.tensor_scalar(gate_w[:, :, :], gate_w[:, :, :], 0.0, None, ALU.max))

            def gate_sum(b):
                after_chained()
                link(dve.tensor_reduce(w_sum[:, :], gate_w[:, :, :], AX.X, ALU.add))
                chained(dve.scalar_tensor_tensor(w_sum[:, :], w_sum[:, :], 0.0, w_sum[:, :], ALU.is_equal, ALU.add))

            def gate_weights(b):
                after_chained()
                link(dve.reciprocal(w_inv[:, :], w_sum[:, :]))
                link(dve.tensor_tensor(gate_w[:, :, :], gate_w[:, :, :],
                                       w_inv[:, :].unsqueeze(2).broadcast_to(wide), ALU.mult))
                if b:
                    dve.wait_ge(turn_full, nth(("hT", b - 1, NT - 1), TURN) + 1)
                for t in range(NT):
                    ins = dve.tensor_tensor(h_w[:, t, :].rearrange("p (e r) -> p e r", e=E),
                                            h_raw[:, t, 0:E * LR].rearrange("p (e r) -> p e r", e=E),
                                            gate_w[:, t, :].unsqueeze(2).broadcast_to([P, E, LR]), ALU.mult)
                ins.then_inc(hw_done, 1)

            def turn(task):
                if task[0] == "max":
                    max_parts(task[1], task[2])
                else:
                    turned(task)

            def rotate(i):
                tiles = 2 if i < 2 else 1
                sin = tables[:, 1:2, :].broadcast_to([P, tiles, S])
                swap = swapped[:, 0:tiles * S].rearrange("p (i t) -> p i t", i=tiles)
                link(dve.tensor_tensor(swap, swap, sin, ALU.mult))
                dve.tensor_tensor(qk[:, 2 * i:2 * i + tiles, :].rearrange("p i t -> p (i t)"), roped_cos[:, 0:tiles * S],
                                  swapped[:, 0:tiles * S], ALU.add).then_inc(rope_done, 1)

            def split(i):
                c = slice(2 * i, min(2 * i + 2, R + 1))
                dve.wait_ge(part_done, 3 * i + 1)
                dve.tensor_tensor(qk[:, c, :], qk[:, c, :], part[0][:, c, :], ALU.subtract).then_inc(rest_done, 1)
                dve.wait_ge(part_done, 3 * i + 2)
                dve.wait_ge(rest_done, i + 1)
                dve.tensor_tensor(part[2][:, c, :], qk[:, c, :], part[1][:, c, :], ALU.subtract).then_inc(part_done, 1)

            for i in range(2):
                dve.memset(k_aug[i][ROWS:ROWS + 2, :, :], 1.0).then_inc(ones, 1)
            dve.memset(v_aug[:, :, :, :, 3 * DH:VC], 1.0).then_inc(ones, 1)
            x_low(0)
            for n in range(KC):
                low(n)
            for i in range(3):
                qkv(0, i)
                rotate(i)
                split(i)
            x_low(1)
            for j in range(STEPS):
                first = j < UNITS
                gates = [b for kind, b, t in dense_of(j - 1) if kind == "adapt"]
                for task in dense_of(j - 1):
                    if task[0] in ("wo", "ffn"):
                        statistics(task)
                for task in turns(j - 1, True):
                    turn(task)
                if first:
                    maximum(j, 0)
                for kind, b, t in dense_of(j - 1):
                    if kind == "qkv":
                        qkv(b, t)
                for b in gates:
                    gate_top(b)
                if 0 <= j - LAG_SPLIT < UNITS:
                    second_part(j - LAG_SPLIT)
                if first:
                    maximum(j, 1)
                for task in turns(j, False):
                    turn(task)
                for b in gates:
                    gate_one(b)
                    gate_inverse(b)
                if 0 <= j - LAG_GATHER < UNITS:
                    gather(j - LAG_GATHER)
                for b in gates:
                    gate_threshold(b)
                if first:
                    maximum(j, 2)
                for b in gates:
                    gate_sum(b)
                for b in gates:
                    gate_weights(b)
                for n in chunk_step:
                    if chunk_step[n] == j:
                        low(n)
                for b in range(2, B):
                    if j == qkv_steps(b)[0] - 1:
                        x_low(b)

        @block.gpsimd
        def _(pool):
            links = [0]

            def link(ins):
                links[0] += 1
                ins.then_inc(pool_chain, 1)
                pool.wait_ge(pool_chain, links[0])

            link(pool.memset(ident[:, :], 1.0))
            link(pool.memset(mask_b[:, :], 0.0))
            link(pool.memset(ident_b[:, :], 1.0))
            diagonal = dict(compare_op=ALU.is_equal, fill=0.0, base=0, pattern=[[-1, P]], channel_multiplier=1)
            pool.affine_select(out=ident[:, :], in_=ident[:, :], **diagonal).then_inc(consts, 1)
            pool.affine_select(out=ident_b[:, :], in_=ident_b[:, :], **diagonal).then_inc(consts, 1)
            pool.affine_select(out=mask_b[:, :], in_=mask_b[:, :], compare_op=ALU.is_ge, fill=MASKED, base=0,
                               pattern=[[-1, P]], channel_multiplier=1).then_inc(consts, 1)
            pool.memset(half[:, :], -0.5)
            pool.wait_ge(small_in, 48)
            pool.tensor_scalar(b_thr[:, :], b_thr[:, :], -1.0, 0.0, ALU.mult, ALU.add).then_inc(consts, 1)

            def qkv(b, i):
                n = 3 * b + i
                tiles = 2 if i < 2 else 1
                w = tiles * S
                pool.wait_ge(swap_done, 2 * n + 2)
                sin = tables[:, 1:2, :].broadcast_to([P, tiles, S])
                swap = swapped[:, 0:w].rearrange("p (i t) -> p i t", i=tiles)
                link(pool.tensor_tensor(swap, swap, sin, ALU.mult))
                pool.wait_ge(acc_free, nth(("qkv", b, i), ACC) + 1)
                if b and i == 0:
                    pool.wait_ge(part_done, 3 * b)
                pool.tensor_tensor(qk[:, 2 * i:2 * i + tiles, :].rearrange("p i t -> p (i t)"), roped_cos[:, 0:w],
                                   swapped[:, 0:w], ALU.add).then_inc(rope_done, 1)

            def v_third(b):
                pool.wait_ge(v_step, 3 * b + 2)
                pool.tensor_tensor(v_aug[:, b % V_RING, :, :, 2 * DH:3 * DH], v_rest[:, :, :, :],
                                   v_aug[:, b % V_RING, :, :, DH:2 * DH], ALU.subtract).then_inc(v_step, 1)

            def split_first(b, i):
                c = slice(2 * i, min(2 * i + 2, R + 1))
                pool.wait_ge(part_done, 9 * b + 3 * i + 1)
                pool.tensor_tensor(qk[:, c, :], qk[:, c, :], part[0][:, c, :], ALU.subtract).then_inc(rest_done, 1)

            def split_second(b, i):
                c = slice(2 * i, min(2 * i + 2, R + 1))
                pool.wait_ge(part_done, 9 * b + 3 * i + 2)
                pool.wait_ge(rest_done, 3 * b + i + 1)
                pool.tensor_tensor(part[2][:, c, :], qk[:, c, :], part[1][:, c, :], ALU.subtract).then_inc(part_done, 1)

            def mask(u):
                i = u % 2
                for c, width in ((0, S), (R * S, P)):
                    pool.wait_ge(exp_done, 2 * u + (2 if c else 1))
                    v = prob[:, i, c:c + R * width].rearrange("p (r q) -> p r q", r=R)[:, :, 0:P]
                    pool.affine_select(out=v, in_=v, compare_op=ALU.is_ge, fill=0.0, base=0,
                                       pattern=[[0, R], [1, P]], channel_multiplier=-1).then_inc(masked, 1)

            def second_part(u):
                i = u % 2
                c = slice(R * S, PCOLS)
                pool.wait_ge(p1_done, u + 1)
                pool.tensor_tensor(p2[:, i, c], prob[:, i, c], p1[:, i, c], ALU.subtract).then_inc(p2_pool, 1)

            def scale(u):
                b, g = divmod(u, G)
                i = u % 2
                pool.wait_ge(o_evac, 2 * u + 2)
                if b and g == 0:
                    pool.wait_ge(turn_full, nth(("attnT", b - 1, NT - 1), TURN) + 1)
                dst = attn[:, :, g * R * DH:(g + 1) * R * DH].rearrange("p t (r d) -> p t r d", r=R)
                src = o_sum[:, i, :, :].rearrange("p (t r) d -> p t r d", t=NT)
                inv = o_inv[:, i, :].rearrange("p (t r) -> p t r", t=NT).unsqueeze(3).broadcast_to([P, NT, R, DH])
                pool.tensor_tensor(dst, src, inv, ALU.mult).then_inc(o_scaled, 1)

            def inverse_deviation(n, t):
                pool.wait_ge(stat_done, n + 1)
                link(pool.tensor_scalar(var_eps[:, t:t + 1], mean_var[:, t, 1:2], EPS, 0.0, ALU.add, ALU.add))
                link(pool.tensor_tensor(rstd[:, t:t + 1], var_eps[:, t:t + 1], half[:, t:t + 1], ALU.pow))
                pool.tensor_scalar(shift[:, t:t + 1], mean_var[:, t, 0:1], rstd[:, t:t + 1], -1.0, ALU.mult,
                                   ALU.mult).then_inc(rstd_done, 1)

            v_third(0)
            for j in range(STEPS):
                if 0 <= j - LAG_SPLIT < UNITS:
                    second_part(j - LAG_SPLIT)
                for kind, b, t in dense_of(j - 1):
                    if kind in ("wo", "ffn"):
                        inverse_deviation(4 * b + t + (2 if kind == "ffn" else 0), t)
                for kind, b, t in dense_of(j - 2):
                    if kind == "wo":
                        pool.wait_ge(ln_done, 4 * b + t + 1)
                        pool.tensor_tensor(s_buf[:, t, :], y_buf[:, t, :], b_row[:, :], ALU.add).then_inc(yb_done, 1)
                if 0 <= j - LAG_ST < UNITS:
                    mask(j - LAG_ST)
                for kind, b, t in dense_of(j - 2):
                    if kind == "qkv":
                        split_first(b, t)
                for kind, b, t in dense_of(j - 1):
                    if kind == "qkv":
                        qkv(b, t)
                if 0 <= j - LAG_GATHER < UNITS:
                    scale(j - LAG_GATHER)
                for kind, b, t in dense_of(j - 2):
                    if kind == "qkv":
                        split_second(b, t)
                        if t == 2:
                            v_third(b)


def kernel(L0_attn_x, L0_attn_w_qkv, L0_attn_w_o, L0_ffn_W_base, L0_ffn_b_base, L0_ffn_W_gate, L0_ffn_W_thr,
           L0_ffn_b_thr, L0_ffn_A_w, L0_ffn_B_w):
    import numpy as np
    import concourse.bacc as bacc
    from concourse.bass_utils import run_bass_kernel_spmd

    x = np.asarray(L0_attn_x)
    half_, freq, group = np.meshgrid(np.arange(2), np.arange(DH // 2), np.arange(G), indexing="ij")
    within = half_ * (DH // 2) + freq
    cols = [((R * group + r) * DH + within).ravel() for r in range(R)]
    cols += [(H * DH + group * DH + within).ravel(), np.arange(H * DH + G * DH, H * DH + 2 * G * DH)]
    cols = np.concatenate(cols)

    def chunked(w):
        return np.ascontiguousarray(w.T.reshape(KC, P, w.shape[0]).transpose(1, 0, 2))

    a_w = np.asarray(L0_ffn_A_w).reshape(E * LR, D)
    adapter = np.concatenate([a_w, np.asarray(L0_ffn_W_gate), np.asarray(L0_ffn_W_thr)[None],
                              np.zeros((1, D), np.float32)])
    inv_freq = (1.0 / 500000.0 ** (np.arange(0, DH, 2, dtype=np.float32) / np.float32(DH))).astype(np.float32)
    angle = np.outer(np.arange(S, dtype=np.float32), inv_freq).astype(np.float32)
    cos, sin = np.cos(angle), np.sin(angle)
    f = freq.ravel()
    sign = np.where(half_.ravel() == 0, -1.0, 1.0).astype(np.float32)
    tab = np.stack([cos[:, f].T, sin[:, f].T * sign[:, None]], axis=1).astype(np.float32)

    arrays = {
        "xT": np.ascontiguousarray(x.reshape(B, S, KC, P).transpose(0, 3, 2, 1)),
        "x": np.ascontiguousarray(x),
        "wqkv": chunked(np.asarray(L0_attn_w_qkv)[cols]),
        "wo": chunked(np.asarray(L0_attn_w_o)),
        "wb": chunked(np.asarray(L0_ffn_W_base)),
        "ag": chunked(adapter).reshape(P, KC * AG),
        "bw": np.ascontiguousarray(np.asarray(L0_ffn_B_w).transpose(0, 2, 1).reshape(E * LR, D)),
        "bbase": np.ascontiguousarray(np.broadcast_to(np.asarray(L0_ffn_b_base), (P, D))),
        "bthr": np.ascontiguousarray(np.broadcast_to(np.asarray(L0_ffn_b_thr), (P, 1))),
        "tab": np.ascontiguousarray(tab),
    }
    nc = bacc.Bacc("TRN2", target_bir_lowering=False, num_devices=1)
    aps = {n: nc.dram_tensor(f"in_{n}", a.shape, mybir.dt.from_np(a.dtype), kind="ExternalInput").ap()
           for n, a in arrays.items()}
    out = nc.dram_tensor("out", (B, S, D), F32, kind="ExternalOutput").ap()
    by_row = "b (t p) d -> b p t d"
    build(nc, aps["xT"], aps["x"].rearrange(by_row, p=P), aps["wqkv"], aps["wo"], aps["wb"], aps["ag"], aps["bw"],
          aps["bbase"], aps["bthr"], aps["tab"], out.rearrange(by_row, p=P))
    r = run_bass_kernel_spmd(nc, [{f"in_{n}": a for n, a in arrays.items()}], core_ids=[0])
    return r.results[0]["out"]
```

```python
from contextlib import ExitStack
import math

import concourse.bass as bass
from concourse import mybir

F32 = mybir.dt.float32
F32R = mybir.dt.float32r
BF16 = mybir.dt.bfloat16
F16 = mybir.dt.float16
ALU = mybir.AluOpType
ACT = mybir.ActivationFunctionType
AX = mybir.AxisListType

P = 128
B, S, D = 4, 256, 512
NT = S // P
KC = D // P
G, R, DH = 8, 4, 16
H = G * R
QK = (R + 1) * P
QKV = QK + G * DH
E, LR = 8, 16
AG = E * LR + E + 2
EPS = 1e-5
SCALING = 2.0
MAX_THRESHOLD = 0.125
SCALE = 1.0 / math.sqrt(DH)
LIFT = math.log(1024.0) / SCALE
Q_PARTS = (0, 1, 0, 1, 2, 0)
K_PARTS = (0, 0, 1, 1, 0, 2)
ROWS = 16 * len(Q_PARTS)
VC = 3 * DH + 1
UNITS = B * G
PCOLS = R * S + R * P
MASKED = -1e37
WARM_UP = 56
PROBS = 3
KEEP = 24
GROUP = 2
GROUPS = G // GROUP
V_RING = 3

LAG_ST, LAG_SPLIT, LAG_PV, LAG_GATHER = 4, 5, 6, 6
STEPS = UNITS + 2 * G


def build(nc, xT, x, wqkv, wo, wb, ag, bw, bbase, bthr, tab, out):
    ctx = ExitStack()
    with ctx:
        def sb(name, shape, dt):
            return ctx.enter_context(nc.sbuf_tensor(name, shape, dt))

        def sem(name):
            return ctx.enter_context(nc.semaphore(name))

        raw = sb("raw", [P, 3 * QKV], F32)
        s_buf, y_buf = (raw[:, i * NT * D:(i + 1) * NT * D].rearrange("p (t d) -> p t d", t=NT) for i in range(2))
        wq_hi, wq_lo = (sb(n, [P, KC, QKV], F32R) for n in ("wq_hi", "wq_lo"))
        wo_hi, wo_lo = (sb(n, [P, KC, D], F32R) for n in ("wo_hi", "wo_lo"))
        wb_hi, wb_lo = (sb(n, [P, KC, D], F32R) for n in ("wb_hi", "wb_lo"))
        ag_hi, ag_lo = (sb(n, [P, KC, AG], F32R) for n in ("ag_hi", "ag_lo"))
        bw_hi, bw_lo = (sb(n, [P, D], F32R) for n in ("bw_hi", "bw_lo"))
        xT_raw = sb("xT_raw", [P, KC, S], F32)
        xT_hi, xT_lo = (sb(n, [P, KC, S], F32R) for n in ("xT_hi", "xT_lo"))
        x_tok = sb("x_tok", [P, NT, D], F32)
        swapped = sb("swapped", [P, 2 * S], F32)
        roped_cos = sb("roped_cos", [P, 2 * S], F32)
        qk = sb("qk", [P, R + 1, S], F32)
        part = [sb(f"part{i}", [P, R + 1, S], BF16) for i in range(3)]
        q_aug = [sb(f"q_aug{i}", [ROWS + 2, H, S], BF16) for i in range(2)]
        k_aug = [sb(f"k_aug{i}", [ROWS + 2, G, S], BF16) for i in range(2)]
        v_aug = sb("v_aug", [P, V_RING, NT, G, VC], BF16)
        v_rest = sb("v_rest", [P, NT, G, DH], F32)
        neg_max = sb("neg_max", [P, 2, NT, GROUP * R], F32)
        m_part = [sb(f"m_part{i}", [NT * GROUP * R, P], BF16) for i in range(2)]
        prob = sb("prob", [P, PROBS, PCOLS], F32)
        p1 = sb("p1", [P, 2, PCOLS], F16)
        p2 = sb("p2", [P, 2, PCOLS], F16)
        o_sum = sb("o_sum", [P, 2, NT * R, DH], F32)
        o_inv = sb("o_inv", [P, 2, NT * R], F32)
        attn = sb("attn", [P, NT, D], F32)
        aT_hi, aT_lo = (sb(n, [P, NT, KC, P], F32R) for n in ("aT_hi", "aT_lo"))
        stats = sb("stats", [P, NT, 6], F32)
        mean_var = sb("mean_var", [P, NT, 2], F32)
        var_eps = sb("var_eps", [P, NT], F32)
        rstd = sb("rstd", [P, NT], F32)
        shift = sb("shift", [P, NT], F32)
        h_raw = sb("h_raw", [P, NT, AG], F32)
        neg_top = sb("neg_top", [P, NT], F32)
        gate_e = sb("gate_e", [P, NT, E], F32)
        gate_c = sb("gate_c", [P, 2, NT], F32)
        gate_r = sb("gate_r", [P, 2, NT], F32)
        gate_t = sb("gate_t", [P, NT], F32)
        gate_w = sb("gate_w", [P, NT, E], F32)
        w_sum = sb("w_sum", [P, NT], F32)
        w_inv = sb("w_inv", [P, NT], F32)
        h_w = sb("h_w", [P, NT, E * LR], F32)
        hT_hi, hT_lo = (sb(n, [P, NT, P], F32R) for n in ("hT_hi", "hT_lo"))
        ident = sb("ident", [P, P], F32)
        ident_b = sb("ident_b", [P, P], BF16)
        mask_b = sb("mask_b", [P, P], BF16)
        b_row = sb("b_row", [P, D], F32)
        b_thr = sb("b_thr", [P, 1], F32)
        tables = sb("tables", [P, 2, S], F32)
        half = sb("half", [P, NT], F32)

        score = [ctx.enter_context(nc.psum_tensor(f"score{i}", [P, 512], F32)) for i in range(2)]
        st_a = ctx.enter_context(nc.psum_tensor("st_a", [P, 1024], F32))
        st_b = ctx.enter_context(nc.psum_tensor("st_b", [P, 512], F32))
        o_ps = ctx.enter_context(nc.psum_tensor("o_ps", [P, 512], F32))
        acc = ctx.enter_context(nc.psum_tensor("acc", [P, 512], F32))
        turn_ps = ctx.enter_context(nc.psum_tensor("turn", [P, 512], F32))
        o_view = o_ps[:, 0:NT * R * VC].rearrange("p (n c) -> p n c", c=VC)

        raw_in = [sem(f"raw_in{i}") for i in range(4)]
        raw_hi = sem("raw_hi")
        raw_lo = sem("raw_lo")
        xT_in, x_in, small_in = sem("xT_in"), sem("x_in"), sem("small_in")
        xT_hi_done, xT_lo_done = sem("xT_hi_done"), sem("xT_lo_done")
        consts, ones = sem("consts"), sem("ones")
        acc_full, acc_free = sem("acc_full"), sem("acc_free")
        turn_full, turn_free = sem("turn_full"), sem("turn_free")
        swap_done, rope_done, rest_done = sem("swap_done"), sem("rope_done"), sem("rest_done")
        v_step = sem("v_step")
        part_done = [sem(f"part_done{i}") for i in range(3)]
        aug_in = [sem(f"aug_in{i}") for i in range(2)]
        max_in = [sem(f"max_in{i}") for i in range(2)]
        score_full, score_free = sem("score_full"), sem("score_free")
        st_full, exp_done, masked, p1_done = sem("st_full"), sem("exp_done"), sem("masked"), sem("p1_done")
        p2_dve, p2_pool = sem("p2_dve"), sem("p2_pool")
        pv_done, o_evac, o_scaled = sem("pv_done"), sem("o_evac"), sem("o_scaled")
        turn_hi = sem("turn_hi")
        stat_done, rstd_done, ln_done, yb_done = sem("stat_done"), sem("rstd_done"), sem("ln_done"), sem("yb_done")
        gate_act, gate_dve, hw_done = sem("gate_act"), sem("gate_dve"), sem("hw_done")
        dve_chain, pool_chain = sem("dve_chain"), sem("pool_chain")
        stored = [sem(f"stored{i}") for i in range(NT)]

        ACC, TURN = ("qkv", "wo", "adapt", "ffn"), ("max", "attnT", "yT", "hT")

        def qkv_steps(b):
            return {1: (-1, 1, 3), 2: (5, 7, 9), 3: (12, 13, 17)}[b]

        def after_attention(b):
            return G * (b + 1) + LAG_GATHER

        def tasks(j):
            todo = []
            for b in range(B):
                if b and j in qkv_steps(b):
                    todo.append(("qkv", b, qkv_steps(b).index(j)))
                t0 = after_attention(b)
                todo += {
                    t0: [("attnT", b, 0)],
                    t0 + 1: [("attnT", b, 1), ("wo", b, 0)],
                    t0 + 2: [("wo", b, 1)],
                    t0 + 3: [("yT", b, 0)],
                    t0 + 4: [("yT", b, 1)],
                    t0 + 5: [("adapt", b, 0)],
                    t0 + 7: [("hT", b, 0), ("hT", b, 1), ("ffn", b, 0)] + [("ffn", b, 1)] * (b == B - 1),
                    t0 + 8: [("ffn", b, 1)] * (b < B - 1),
                }.get(j, [])
            if j % GROUP == 0 and 0 < j <= UNITS:
                todo.insert(0, ("max", (j - 1) // G, (j // GROUP - 1) % GROUPS))
            return todo

        def turns(j, late):
            now = [t for t in tasks(j) if t[0] in TURN]
            return [t for t in now if (t[0] + str(t[2]) in ("attnT0", "yT1") or t[:3:2] == ("hT", 1) and t[1] < B - 1) == late]

        def dense_of(j):
            return [t for t in tasks(j) if t[0] in ACC]

        prologue = [("qkv", 0, i) for i in range(3)]
        order = prologue + [t for j in range(-1, STEPS) for t in dense_of(j)]
        order += [t for j in range(STEPS) for late in (False, True) for t in turns(j, late)]

        def nth(task, kinds):
            return sum(t[0] in kinds for t in order[:order.index(task)])

        chunks = [(wqkv[:, k, :], QKV, wq_hi[:, k, :], wq_lo[:, k, :], 1.0) for k in range(KC)]
        chunks += [(wo[:, k, :], D, wo_hi[:, k, :], wo_lo[:, k, :], 1.0) for k in range(KC)]
        chunks += [(wb[:, k, :], D, wb_hi[:, k, :], wb_lo[:, k, :], 1.0) for k in range(KC)]
        chunks += [(ag, KC * AG, ag_hi[:, :, :].rearrange("p k n -> p (k n)"),
                    ag_lo[:, :, :].rearrange("p k n -> p (k n)"), 1.0)]
        chunks += [(bw, D, bw_hi[:, :], bw_lo[:, :], SCALING)]
        raw_slot = [raw[:, i * QKV:(i + 1) * QKV] for i in range(3)] + [x_tok[:, :, :].rearrange("p t d -> p (t d)")]

        def slot(n):
            return n if n < 4 else (n - 4) % 3

        def arrived(n):
            return 16 * (1 if n < 4 else (n - 4) // 3 + 2)

        chunk_step = {n: 1 + (n - KC) for n in range(KC, len(chunks))}

        tail = [t for j in range(UNITS + 1, STEPS) for t in dense_of(j)]

        def bank(task):
            if task[:2] == ("qkv", 0):
                return (acc, st_b, o_ps)[task[2]]
            return (acc, *score)[tail.index(task) % 3] if task in tail else acc

        block = ctx.enter_context(nc.Block())

        @block.sync
        def _(sp):
            def load_chunk(n):
                if n >= 4:
                    sp.wait_ge(raw_lo, n - 3 if n < 7 else n - 2)
                sp.dma_start(raw_slot[slot(n)][:, 0:chunks[n][1]], chunks[n][0]).then_inc(raw_in[slot(n)], 16)

            def load_xT(b):
                if b:
                    sp.wait_ge(xT_lo_done, b)
                sp.dma_start(xT_raw[:, :, :], xT[b]).then_inc(xT_in, 16)

            def fill_aug(b):
                i = b % 2
                if b >= 2:
                    sp.wait_ge(st_full, 2 * G * (b - 1))
                for n in range(3):
                    sp.wait_ge(part_done[n], 3 * (b + 1))
                    for s in range(len(Q_PARTS)):
                        if Q_PARTS[s] == n:
                            sp.dma_start(q_aug[i][16 * s:16 * s + 16, :, :],
                                         part[n][:, 0:R, :]).then_inc(aug_in[i], 16)
                        if K_PARTS[s] == n:
                            sp.dma_start(k_aug[i][16 * s:16 * s + 16, :, :],
                                         part[n][:, R, :]).then_inc(aug_in[i], 16)

            def fill_max(b, k):
                n = GROUPS * b + k
                sp.wait_ge(turn_free, nth(("max", b, k), TURN) + 1)
                for c in range(2):
                    for t in range(NT):
                        sp.dma_start(q_aug[b % 2][ROWS + c:ROWS + c + 1, GROUP * R * k:GROUP * R * (k + 1), t * P:(t + 1) * P],
                                     m_part[c][t * GROUP * R:(t + 1) * GROUP * R, :]).then_inc(max_in[n % 2], 16)

            load_xT(0)
            for n in range(4):
                load_chunk(n)
            sp.dma_start(tables[:, :, :], tab).then_inc(small_in, 16)
            sp.dma_start(b_row[:, :], bbase).then_inc(small_in, 16)
            sp.dma_start(b_thr[:, :], bthr).then_inc(small_in, 16)
            load_xT(1)
            fill_aug(0)
            for j in range(STEPS):
                for n in chunk_step:
                    if chunk_step[n] == j + 1:
                        load_chunk(n)
                for b in range(B):
                    if b > 1 and j == max(qkv_steps(b)[0] - 4, 0):
                        load_xT(b)
                    if j == G * b + 12:
                        if b:
                            sp.wait_ge(acc_free, nth(("wo", b - 1, 1), ACC) + 1)
                        sp.dma_start(x_tok[:, :, :], x[b]).then_inc(x_in, 16)
                for kind, b, t in tasks(j):
                    if kind == "max":
                        fill_max(b, t)
                for b in range(1, B):
                    if j == max(G * (b - 1) + LAG_ST - 1, 5):
                        fill_aug(b)
                for kind, b, t in dense_of(j - 1):
                    if kind == "ffn":
                        sp.wait_ge(ln_done, 4 * b + 2 + t + 1)
                        sp.dma_start(out[b][:, t, :], s_buf[:, t, :]).then_inc(stored[t], 16)
            for t in range(NT):
                sp.wait_ge(stored[t], 16 * B)

        @block.tensor
        def _(pe):
            def take(task, kinds, full, free):
                n = nth(task, kinds)
                if n:
                    pe.wait_ge(free, n)

            def three(dst, a_hi, a_lo, b_hi, b_lo, first, last):
                pe.matmul(dst, a_hi, b_hi, start=first, stop=False)
                pe.matmul(dst, a_hi, b_lo, start=False, stop=False)
                return pe.matmul(dst, a_lo, b_hi, start=False, stop=last)

            def dense_quarter(task, q):
                kind, b, t = task
                acc = bank(task)
                if q == 0:
                    if task == ("qkv", 1, 0):
                        pe.wait_ge(acc_free, 1)
                    elif task in tail[1:3]:
                        pe.wait_ge(score_free, 3 * UNITS)
                    elif task in tail[3:]:
                        pe.wait_ge(acc_free, nth(task, ACC) - 2)
                    elif (kind, b) != ("qkv", 0):
                        pe.wait_ge(acc_free, nth(task, ACC))
                if kind == "qkv":
                    if q == 0 and t == 0:
                        pe.wait_ge(xT_hi_done, b + 1)
                        pe.wait_ge(xT_lo_done, b + 1)
                    if t < 2:
                        tile, ks, dst = 2 * t + q // 2, (2 * (q % 2), 2 * (q % 2) + 1), acc[:, (q // 2) * S:(q // 2 + 1) * S]
                    elif q < 2:
                        tile, ks, dst = R, (2 * q, 2 * q + 1), acc[:, 0:S]
                    if t < 2 or q < 2:
                        for k in ks:
                            if b == 0 and t == 0 and q < 2:
                                pe.wait_ge(raw_hi, k + 1)
                                pe.wait_ge(raw_lo, k + 1)
                            c = slice(tile * P, (tile + 1) * P)
                            last = three(dst, wq_hi[:, k, c], wq_lo[:, k, c], xT_hi[:, k, :], xT_lo[:, k, :],
                                         k == 0, k == KC - 1)
                    else:
                        for k in range(KC):
                            c = slice((q - 2) * P, (q - 1) * P)
                            last = three(acc[:, S + (q - 2) * P:S + (q - 1) * P], xT_hi[:, k, c], xT_lo[:, k, c],
                                         wq_hi[:, k, QK:QKV], wq_lo[:, k, QK:QKV], k == 0, k == KC - 1)
                elif kind == "adapt":
                    tt = q // 2
                    pe.wait_ge(turn_free, nth(("yT", b, tt), TURN) + 1)
                    for k in (2 * (q % 2), 2 * (q % 2) + 1):
                        if b == 0 and q == 0:
                            pe.wait_ge(raw_lo, 3 * KC + 1)
                        last = three(acc[:, tt * S:tt * S + AG], aT_hi[:, tt, k, :], aT_lo[:, tt, k, :],
                                     ag_hi[:, k, :], ag_lo[:, k, :], k == 0, k == KC - 1)
                else:
                    if q == 0:
                        pe.wait_ge(turn_free, nth(("attnT" if kind == "wo" else "yT", b, t), TURN) + 1)
                        if b == 0 and t == 0:
                            pe.wait_ge(raw_lo, 2 * KC if kind == "wo" else 3 * KC + 2)
                    hi, lo = (wo_hi, wo_lo) if kind == "wo" else (wb_hi, wb_lo)
                    last = three(acc[:, :], aT_hi[:, t, q, :], aT_lo[:, t, q, :], hi[:, q, :], lo[:, q, :],
                                 q == 0, q == KC - 1 and kind == "wo")
                    if kind == "ffn" and q == KC - 1 and b < B - 1:
                        pe.wait_ge(turn_free, nth(("hT", b, t), TURN) + 1)
                        last = three(acc[:, :], hT_hi[:, t, :], hT_lo[:, t, :], bw_hi[:, :], bw_lo[:, :], False, True)
                if q == 3 and not (kind == "ffn" and b == B - 1):
                    last.then_inc(acc_full, 1)

            def adapters(t):
                pe.wait_ge(turn_free, nth(("hT", B - 1, t), TURN) + 1)
                three(bank(("ffn", B - 1, t))[:, :], hT_hi[:, t, :], hT_lo[:, t, :], bw_hi[:, :], bw_lo[:, :],
                      False, True).then_inc(acc_full, 1)

            def scores(u, n):
                b, g = divmod(u, G)
                if g == 0 and n == 0:
                    pe.wait_ge(aug_in[b % 2], 16 * 12 * (b // 2 + 1))
                    if b == 0:
                        pe.wait_ge(consts, 3)
                q, k = q_aug[b % 2], k_aug[b % 2]
                t, heads = ((0, (0, 1, 2, 3)), (1, (0, 1)), (1, (2, 3)))[n]
                use = 3 * u + n
                if use >= 2:
                    pe.wait_ge(score_free, use - 1)
                width = (t + 1) * P
                for i, r in enumerate(heads):
                    pe.matmul(score[use % 2][:, i * width:(i + 1) * width],
                              q[0:ROWS, R * g + r, t * P:(t + 1) * P], k[0:ROWS, g, 0:width],
                              start=True, stop=False)
                    last = pe.matmul(score[use % 2][:, (i + 1) * width - P:(i + 1) * width],
                                     ident_b[:, :], mask_b[:, :], start=False, stop=True)
                last.then_inc(score_full, 1)

            def scores_t(u, late):
                b, g = divmod(u, G)
                if g % GROUP == 0 and not late:
                    n = GROUPS * b + g // GROUP
                    pe.wait_ge(max_in[n % 2], 64 * (n // 2 + 1))
                if u == 0:
                    pe.wait_ge(ones, 2)
                if u:
                    pe.wait_ge(exp_done, 2 * u if late else 2 * u - 1)
                q, k = q_aug[b % 2], k_aug[b % 2]
                if late:
                    last = pe.matmul(st_b[:, :], k[:, g, P:S], q[:, R * g:R * g + R, P:S], start=True, stop=True)
                else:
                    for i in range(2):
                        last = pe.matmul(st_a[:, i * 512:(i + 1) * 512], k[:, g, 0:P],
                                         q[:, R * g + 2 * i:R * g + 2 * i + 2, :], start=True, stop=True)
                last.then_inc(st_full, 1)

            def values(u):
                b, g = divmod(u, G)
                i = u % 2
                pe.wait_ge(p1_done, u + 1)
                pe.wait_ge(p2_dve, u + 1)
                pe.wait_ge(p2_pool, u + 1)
                if g == 0:
                    pe.wait_ge(v_step, 3 * (b + 1))
                if u == 0:
                    pe.wait_ge(ones, 3)
                if u:
                    pe.wait_ge(o_evac, 2 * u)
                v = [v_aug[:, b % V_RING, t, g, :] for t in range(NT)]
                for t in range(NT):
                    for r in range(R):
                        dst = o_view[:, R * t + r, :]
                        at = [(r * S + t * P, 0)] + ([(R * S + r * P, 1)] if t else [])
                        for c, kb in at:
                            for pp in (p1, p2):
                                last = pe.matmul(dst, pp[:, i, c:c + P], v[kb], start=(kb == 0 and pp is p1),
                                                 stop=((c, kb) == at[-1] and pp is p2))
                last.then_inc(pv_done, 1)

            def max_turn(b, k):
                take(("max", b, k), TURN, turn_full, turn_free)
                pe.wait_ge(score_free, 3 * GROUP * (GROUPS * b + k + 1))
                pe.transpose(turn_ps[0:NT * GROUP * R, 0:P], neg_max[:, (GROUPS * b + k) % 2, :, :].rearrange("p t h -> p (t h)"),
                             ident[:, :]).then_inc(turn_full, 1)

            def turn_rows(task, src, ready, count):
                take(task, TURN, turn_full, turn_free)
                pe.wait_ge(ready, count)
                for k in range(KC):
                    last = pe.transpose(turn_ps[:, k * P:(k + 1) * P], src[:, k * P:(k + 1) * P], ident[:, :])
                last.then_inc(turn_full, 1)

            def turn(task):
                kind, b, t = task
                if kind == "max":
                    max_turn(b, t)
                if kind == "attnT":
                    turn_rows(task, attn[:, t, :], o_scaled, G * (b + 1))
                if kind == "yT":
                    turn_rows(task, y_buf[:, t, :], ln_done, 4 * b + t + 1)
                if kind == "hT":
                    take(task, TURN, turn_full, turn_free)
                    pe.wait_ge(hw_done, b + 1)
                    pe.transpose(turn_ps[:, 0:P], h_w[:, t, :], ident[:, :]).then_inc(turn_full, 1)

            def keep_warm(j):
                if j < UNITS + LAG_ST:
                    pe.wait_ge(acc_free, sum(t[0] in ACC for i in range(-1, j) for t in tasks(i)) + 3)
                else:
                    pe.wait_ge(exp_done, 2 * UNITS)
                spare = acc if j < UNITS + LAG_ST else st_a
                for _ in range(KEEP):
                    pe.matmul(spare[:, 0:P], ident_b[:, :], ident_b[:, :], start=True, stop=True)

            def dense(j, q):
                for task in dense_of(j):
                    if task[:2] != ("ffn", B - 1):
                        dense_quarter(task, q)

            pe.wait_ge(consts, 2)
            for _ in range(WARM_UP):
                pe.matmul(score[0][:, 0:P], ident_b[:, :], ident_b[:, :], start=True, stop=True)
            for i in range(3):
                for q in range(4):
                    dense_quarter(("qkv", 0, i), q)
            for q in range(4):
                dense(-1, q)
            for j in range(STEPS):
                first, second, third = j < UNITS, 0 <= j - LAG_ST < UNITS, 0 <= j - LAG_PV < UNITS
                if second:
                    scores_t(j - LAG_ST, False)
                    scores_t(j - LAG_ST, True)
                if first:
                    scores(j, 0)
                    scores(j, 1)
                if third:
                    values(j - LAG_PV)
                for task in turns(j, False):
                    turn(task)
                dense(j, 0)
                dense(j, 1)
                if first:
                    scores(j, 2)
                dense(j, 2)
                dense(j, 3)
                if j == after_attention(B - 1) + 6:
                    for t in range(NT):
                        for q in range(4):
                            dense_quarter(("ffn", B - 1, t), q)
                elif j == after_attention(B - 1) + 7:
                    for t in range(NT):
                        adapters(t)
                elif not dense_of(j):
                    keep_warm(j)
                for task in turns(j, True):
                    turn(task)

        @block.scalar
        def _(act):
            def high(n):
                act.wait_ge(raw_in[slot(n)], arrived(n))
                _, cols, hi, _, scale = chunks[n]
                act.activation(hi, raw_slot[slot(n)][:, 0:cols], ACT.Copy, scale=scale).then_inc(raw_hi, 1)

            def x_high(b):
                act.wait_ge(xT_in, 16 * (b + 1))
                if b:
                    act.wait_ge(acc_full, nth(("qkv", b - 1, 2), ACC) + 1)
                act.activation(xT_hi[:, :, :], xT_raw[:, :, :], ACT.Copy).then_inc(xT_hi_done, 1)

            def qkv(b, i):
                acc = bank(("qkv", b, i))
                act.wait_ge(acc_full, nth(("qkv", b, i), ACC) + 1)
                n = 3 * b + i
                if n:
                    act.wait_ge(rope_done, n)
                w = 2 * S if i < 2 else S
                act.activation(swapped[0:64, 0:w], acc[64:128, 0:w], ACT.Copy).then_inc(swap_done, 1)
                act.activation(swapped[64:128, 0:w], acc[0:64, 0:w], ACT.Copy).then_inc(swap_done, 1)
                if i == 2:
                    if b >= V_RING:
                        act.wait_ge(pv_done, G * (b - V_RING + 1))
                    v = v_aug[:, b % V_RING, :, :, :]
                    src = acc[:, S:2 * S].rearrange("p (t g d) -> p t g d", t=NT, g=G)
                    act.activation(v[:, :, :, 0:DH], src, ACT.Copy).then_inc(v_step, 1)

            def v_second(b):
                act.wait_ge(acc_free, nth(("qkv", b, 2), ACC) + 1)
                act.activation(v_aug[:, b % V_RING, :, :, DH:2 * DH], v_rest[:, :, :, :], ACT.Copy).then_inc(v_step, 1)

            def exps(u, late):
                i = u % PROBS
                if not late:
                    if u >= PROBS:
                        act.wait_ge(p2_dve, u - PROBS + 1)
                        act.wait_ge(p2_pool, u - PROBS + 1)
                    act.wait_ge(st_full, 2 * u + 1)
                    act.activation(prob[:, i, 0:R * S], st_a[:, :], ACT.Exp, scale=SCALE).then_inc(exp_done, 1)
                else:
                    act.wait_ge(st_full, 2 * u + 2)
                    act.activation(prob[:, i, R * S:PCOLS], st_b[:, :], ACT.Exp, scale=SCALE).then_inc(exp_done, 1)

            def first_part(u):
                i = u % 2
                act.wait_ge(masked, 2 * u + 2)
                if u >= 2:
                    act.wait_ge(pv_done, u - 1)
                act.activation(p1[:, i, :], prob[:, u % PROBS, :], ACT.Copy).then_inc(p1_done, 1)

            def turned(task):
                kind, b, t = task
                act.wait_ge(turn_full, nth(task, TURN) + 1)
                if kind == "attnT" and b:
                    act.wait_ge(acc_full, nth(("ffn", b - 1, t), ACC) + 1)
                if kind == "yT":
                    act.wait_ge(acc_full, nth(("wo", b, t), ACC) + 1)
                act.activation(aT_hi[:, t, :, :].rearrange("p k q -> p (k q)"), turn_ps[:, :], ACT.Copy).then_inc(turn_hi, 1)

            def h_turned(task):
                kind, b, t = task
                act.wait_ge(turn_full, nth(task, TURN) + 1)
                if b:
                    act.wait_ge(acc_full, nth(("ffn", b - 1, t), ACC) + 1)
                act.activation(hT_hi[:, t, :], turn_ps[:, 0:P], ACT.Copy).then_inc(turn_hi, 1)

            def adapt(task):
                kind, b, t = task
                act.wait_ge(acc_full, nth(task, ACC) + 1)
                if b:
                    act.wait_ge(hw_done, b)
                act.activation(h_raw[:, :, :], bank(task)[:, :].rearrange("p (t n) -> p t n", t=NT)[:, :, 0:AG],
                               ACT.Copy).then_inc(acc_free, 1)

            def normalize(n, src, dst, t):
                act.wait_ge(rstd_done, n + 1)
                act.activation(dst, src, ACT.Identity, bias=shift[:, t:t + 1],
                               scale=rstd[:, t:t + 1]).then_inc(ln_done, 1)

            def turn(task):
                if task[0] in ("attnT", "yT"):
                    turned(task)
                if task[0] == "hT":
                    h_turned(task)

            def gate(b):
                act.wait_ge(gate_dve, b + 1)
                if b == 0:
                    act.wait_ge(consts, 4)
                for t in range(NT):
                    act.activation(gate_e[:, t, :], h_raw[:, t, E * LR:E * LR + E], ACT.Exp, bias=neg_top[:, t:t + 1],
                                   accum_out=gate_c[:, 0, t:t + 1]).then_inc(gate_act, 1)
                act.activation(gate_c[:, 1, :], h_raw[:, :, AG - 2], ACT.Exp, scale=-1.0,
                               bias=b_thr[:, 0:1]).then_inc(gate_act, 1)

            def tiles_of(i):
                return slice(2 * i, min(2 * i + 2, R + 1))

            def split_first(b, i):
                act.wait_ge(rope_done, 3 * b + i + 1)
                if b:
                    act.wait_ge(aug_in[(b - 1) % 2], 16 * 12 * ((b - 1) // 2 + 1))
                act.activation(part[0][:, tiles_of(i), :], qk[:, tiles_of(i), :], ACT.Copy).then_inc(part_done[0], 1)

            def split_second(b, i):
                act.wait_ge(rest_done, 3 * b + i + 1)
                act.activation(part[1][:, tiles_of(i), :], qk[:, tiles_of(i), :], ACT.Copy).then_inc(part_done[1], 1)

            def split_probabilities(j):
                if 0 <= j - LAG_SPLIT < UNITS:
                    first_part(j - LAG_SPLIT)

            x_high(0)
            for n in range(KC):
                high(n)
            qkv(0, 0)
            split_first(0, 0)
            qkv(0, 1)
            split_second(0, 0)
            split_first(0, 1)
            qkv(0, 2)
            split_second(0, 1)
            x_high(1)
            split_first(0, 2)
            split_second(0, 2)
            v_second(0)
            for j in range(STEPS):
                before = dense_of(j - 1)
                for task in turns(j - 1, True):
                    turn(task)
                if j < UNITS:
                    split_probabilities(j)
                for kind, b, t in before:
                    if kind == "qkv":
                        qkv(b, t)
                    if kind == "adapt":
                        adapt((kind, b, t))
                if 0 <= j - LAG_ST < UNITS:
                    exps(j - LAG_ST, False)
                if 0 <= j - LAG_ST < UNITS:
                    exps(j - LAG_ST, True)
                if j >= UNITS:
                    split_probabilities(j)
                for task in turns(j, False):
                    turn(task)
                for kind, b, t in dense_of(j - 2):
                    if kind == "qkv":
                        split_first(b, t)
                for kind, b, t in before:
                    if kind == "wo":
                        normalize(4 * b + t, s_buf[:, t, :], y_buf[:, t, :], t)
                    if kind == "ffn":
                        normalize(4 * b + 2 + t, y_buf[:, t, :], s_buf[:, t, :], t)
                    if kind == "adapt":
                        gate(b)
                    if kind == "qkv" and t == 2:
                        v_second(b)
                for kind, b, t in dense_of(j - 2):
                    if kind == "qkv":
                        split_second(b, t)
                for n in chunk_step:
                    if chunk_step[n] == j:
                        high(n)
                for b in range(2, B):
                    if j == qkv_steps(b)[0] - 1:
                        x_high(b)

        @block.vector
        def _(dve):
            links = [0]

            def link(ins):
                links[0] += 1
                ins.then_inc(dve_chain, 1)
                dve.wait_ge(dve_chain, links[0])

            def low(n):
                dve.wait_ge(raw_hi, n + 1)
                _, cols, hi, lo, scale = chunks[n]
                dve.scalar_tensor_tensor(lo, raw_slot[slot(n)][:, 0:cols], scale, hi.bitcast(F32), ALU.mult,
                                         ALU.subtract).then_inc(raw_lo, 1)

            def x_low(b):
                dve.wait_ge(xT_hi_done, b + 1)
                dve.tensor_tensor(xT_lo[:, :, :], xT_raw[:, :, :], xT_hi[:, :, :].bitcast(F32),
                                  ALU.subtract).then_inc(xT_lo_done, 1)

            def qkv(b, i):
                n = 3 * b + i
                acc = bank(("qkv", b, i))
                dve.wait_ge(acc_full, nth(("qkv", b, i), ACC) + 1)
                if n == 0:
                    dve.wait_ge(small_in, 48)
                if n:
                    dve.wait_ge(rope_done, n)
                dve.wait_ge(swap_done, 2 * n + 2)
                if i == 2:
                    dve.wait_ge(v_step, 3 * b + 1)
                tiles = 2 if i < 2 else 1
                cos = tables[:, 0:1, :].broadcast_to([P, tiles, S])
                ins = dve.tensor_tensor(roped_cos[:, 0:tiles * S].rearrange("p (i t) -> p i t", i=tiles),
                                        acc[:, 0:tiles * S].rearrange("p (i t) -> p i t", i=tiles), cos, ALU.mult)
                if i == 2:
                    ins = dve.tensor_tensor(v_rest[:, :, :, :],
                                            acc[:, S:2 * S].rearrange("p (t g d) -> p t g d", t=NT, g=G),
                                            v_aug[:, b % V_RING, :, :, 0:DH], ALU.subtract)
                ins.then_inc(acc_free, 1)

            def maximum(u, i):
                b, g = divmod(u, G)
                n = u // GROUP
                if u % GROUP == 0 and i == 0 and n >= 2:
                    dve.wait_ge(turn_full, nth(("max", (n - 2) // GROUPS, (n - 2) % GROUPS), TURN) + 1)
                t, first, heads = ((0, 0, 4), (1, 0, 2), (1, 2, 2))[i]
                use = 3 * u + i
                dve.wait_ge(score_full, use + 1)
                at = R * (g % GROUP) + first
                dve.tensor_reduce(neg_max[:, n % 2, t, at:at + heads],
                                  score[use % 2][:, :].rearrange("p (h k) -> p h k", h=heads), AX.X, ALU.max,
                                  negate=True).then_inc(score_free, 1)

            def max_parts(b, k):
                n = GROUPS * b + k
                dve.wait_ge(turn_full, nth(("max", b, k), TURN) + 1)
                if n:
                    dve.wait_ge(max_in[(n - 1) % 2], 64 * ((n - 1) // 2 + 1))
                src = turn_ps[0:NT * GROUP * R, 0:P]
                link(dve.tensor_scalar(m_part[0][:, :], src, LIFT, None, ALU.add))
                dve.scalar_tensor_tensor(m_part[1][:, :], src, LIFT, m_part[0][:, :], ALU.add,
                                         ALU.subtract).then_inc(turn_free, 1)

            def second_part(u):
                i = u % 2
                dve.wait_ge(p1_done, u + 1)
                c = slice(0, R * S)
                dve.tensor_tensor(p2[:, i, c], prob[:, u % PROBS, c], p1[:, i, c], ALU.subtract).then_inc(p2_dve, 1)

            def gather(u):
                i = u % 2
                dve.wait_ge(pv_done, u + 1)
                if u >= 2:
                    dve.wait_ge(o_scaled, u - 1)
                dve.tensor_reduce(o_sum[:, i, :, :], o_view[:, :, 0:3 * DH].rearrange("p n (c d) -> p n d c", c=3),
                                  AX.X, ALU.add).then_inc(o_evac, 1)
                dve.reciprocal(o_inv[:, i, :], o_view[:, :, 3 * DH]).then_inc(o_evac, 1)

            def turned(task):
                kind, b, t = task
                dve.wait_ge(turn_hi, nth(task, ("attnT", "yT", "hT")) + 1)
                if kind == "hT":
                    hi, lo, src = hT_hi[:, t, :], hT_lo[:, t, :], turn_ps[:, 0:P]
                else:
                    hi, lo = (x_[:, t, :, :].rearrange("p k q -> p (k q)") for x_ in (aT_hi, aT_lo))
                    src = turn_ps[:, :]
                dve.tensor_tensor(lo, src, hi.bitcast(F32), ALU.subtract).then_inc(turn_free, 1)

            def statistics(task):
                kind, b, t = task
                dve.wait_ge(acc_full, nth(task, ACC) + 1)
                if kind == "wo":
                    dve.wait_ge(x_in, 16 * (b + 1))
                    if b:
                        dve.wait_ge(stored[t], 16 * b)
                    res, dst = x_tok[:, t, :], s_buf[:, t, :]
                else:
                    dve.wait_ge(yb_done, NT * b + t + 1)
                    res, dst = s_buf[:, t, :], y_buf[:, t, :]
                dve.tensor_tensor(dst, bank(task)[:, :], res, ALU.add).then_inc(acc_free, 1)
                dve.wait_ge(acc_free, nth(task, ACC) + 1)
                link(dve.bn_stats(stats[:, t, :], dst))
                dve.bn_aggr(mean_var[:, t, :], stats[:, t, :]).then_inc(stat_done, 1)

            def chained(ins):
                links[0] += 1
                ins.then_inc(dve_chain, 1)

            def after_chained():
                dve.wait_ge(dve_chain, links[0])

            wide = [P, NT, E]

            def gate_top(b):
                dve.wait_ge(acc_free, nth(("adapt", b, 0), ACC) + 1)
                dve.tensor_reduce(neg_top[:, :], h_raw[:, :, E * LR:E * LR + E], AX.X, ALU.max,
                                  negate=True).then_inc(gate_dve, 1)

            def gate_one(b):
                dve.wait_ge(gate_act, 3 * (b + 1))
                chained(dve.tensor_scalar(gate_c[:, 1, :], gate_c[:, 1, :], 1.0, None, ALU.add))

            def gate_inverse(b):
                after_chained()
                link(dve.reciprocal(gate_r[:, :, :], gate_c[:, :, :]))
                dve.tensor_scalar(gate_t[:, :], gate_r[:, 1, :], MAX_THRESHOLD, None, ALU.mult)
                chained(dve.tensor_tensor(gate_w[:, :, :], gate_e[:, :, :],
                                          gate_r[:, 0, :].unsqueeze(2).broadcast_to(wide), ALU.mult))

            def gate_threshold(b):
                after_chained()
                link(dve.tensor_tensor(gate_w[:, :, :], gate_w[:, :, :],
                                       gate_t[:, :].unsqueeze(2).broadcast_to(wide), ALU.subtract))
                chained(dve.tensor_scalar(gate_w[:, :, :], gate_w[:, :, :], 0.0, None, ALU.max))

            def gate_sum(b):
                after_chained()
                link(dve.tensor_reduce(w_sum[:, :], gate_w[:, :, :], AX.X, ALU.add))
                chained(dve.scalar_tensor_tensor(w_sum[:, :], w_sum[:, :], 0.0, w_sum[:, :], ALU.is_equal, ALU.add))

            def gate_weights(b):
                after_chained()
                link(dve.reciprocal(w_inv[:, :], w_sum[:, :]))
                link(dve.tensor_tensor(gate_w[:, :, :], gate_w[:, :, :],
                                       w_inv[:, :].unsqueeze(2).broadcast_to(wide), ALU.mult))
                if b:
                    dve.wait_ge(turn_full, nth(("hT", b - 1, NT - 1), TURN) + 1)
                for t in range(NT):
                    ins = dve.tensor_tensor(h_w[:, t, :].rearrange("p (e r) -> p e r", e=E),
                                            h_raw[:, t, 0:E * LR].rearrange("p (e r) -> p e r", e=E),
                                            gate_w[:, t, :].unsqueeze(2).broadcast_to([P, E, LR]), ALU.mult)
                ins.then_inc(hw_done, 1)

            def turn(task):
                if task[0] == "max":
                    max_parts(task[1], task[2])
                else:
                    turned(task)

            def rotate(i):
                tiles = 2 if i < 2 else 1
                sin = tables[:, 1:2, :].broadcast_to([P, tiles, S])
                swap = swapped[:, 0:tiles * S].rearrange("p (i t) -> p i t", i=tiles)
                link(dve.tensor_tensor(swap, swap, sin, ALU.mult))
                dve.tensor_tensor(qk[:, 2 * i:2 * i + tiles, :].rearrange("p i t -> p (i t)"), roped_cos[:, 0:tiles * S],
                                  swapped[:, 0:tiles * S], ALU.add).then_inc(rope_done, 1)

            def split_first(i):
                c = slice(2 * i, min(2 * i + 2, R + 1))
                dve.wait_ge(part_done[0], i + 1)
                dve.tensor_tensor(qk[:, c, :], qk[:, c, :], part[0][:, c, :], ALU.subtract).then_inc(rest_done, 1)

            for i in range(2):
                dve.memset(k_aug[i][ROWS:ROWS + 2, :, :], 1.0).then_inc(ones, 1)
            dve.memset(v_aug[:, :, :, :, 3 * DH:VC], 1.0).then_inc(ones, 1)
            x_low(0)
            for n in range(KC):
                low(n)
            for i in range(3):
                qkv(0, i)
                rotate(i)
                split_first(i)
            x_low(1)
            for j in range(STEPS):
                first = j < UNITS
                gates = [b for kind, b, t in dense_of(j - 1) if kind == "adapt"]
                for task in dense_of(j - 1):
                    if task[0] in ("wo", "ffn"):
                        statistics(task)
                for task in turns(j - 1, True):
                    turn(task)
                if first:
                    maximum(j, 0)
                for kind, b, t in dense_of(j - 1):
                    if kind == "qkv":
                        qkv(b, t)
                for b in gates:
                    gate_top(b)
                if 0 <= j - LAG_SPLIT < UNITS:
                    second_part(j - LAG_SPLIT)
                if first:
                    maximum(j, 1)
                for task in turns(j, False):
                    turn(task)
                for b in gates:
                    gate_one(b)
                    gate_inverse(b)
                if 0 <= j - LAG_GATHER < UNITS:
                    gather(j - LAG_GATHER)
                for b in gates:
                    gate_threshold(b)
                if first:
                    maximum(j, 2)
                for b in gates:
                    gate_sum(b)
                for b in gates:
                    gate_weights(b)
                for n in chunk_step:
                    if chunk_step[n] == j:
                        low(n)
                for b in range(2, B):
                    if j == qkv_steps(b)[0] - 1:
                        x_low(b)

        @block.gpsimd
        def _(pool):
            links = [0]

            def link(ins):
                links[0] += 1
                ins.then_inc(pool_chain, 1)
                pool.wait_ge(pool_chain, links[0])

            link(pool.memset(ident[:, :], 1.0))
            link(pool.memset(mask_b[:, :], 0.0))
            link(pool.memset(ident_b[:, :], 1.0))
            diagonal = dict(compare_op=ALU.is_equal, fill=0.0, base=0, pattern=[[-1, P]], channel_multiplier=1)
            pool.affine_select(out=ident[:, :], in_=ident[:, :], **diagonal).then_inc(consts, 1)
            pool.affine_select(out=ident_b[:, :], in_=ident_b[:, :], **diagonal).then_inc(consts, 1)
            pool.affine_select(out=mask_b[:, :], in_=mask_b[:, :], compare_op=ALU.is_ge, fill=MASKED, base=0,
                               pattern=[[-1, P]], channel_multiplier=1).then_inc(consts, 1)
            pool.memset(half[:, :], -0.5)
            pool.wait_ge(small_in, 48)
            pool.tensor_scalar(b_thr[:, :], b_thr[:, :], -1.0, 0.0, ALU.mult, ALU.add).then_inc(consts, 1)

            def qkv(b, i):
                n = 3 * b + i
                tiles = 2 if i < 2 else 1
                w = tiles * S
                pool.wait_ge(swap_done, 2 * n + 2)
                sin = tables[:, 1:2, :].broadcast_to([P, tiles, S])
                swap = swapped[:, 0:w].rearrange("p (i t) -> p i t", i=tiles)
                link(pool.tensor_tensor(swap, swap, sin, ALU.mult))
                pool.wait_ge(acc_free, nth(("qkv", b, i), ACC) + 1)
                if i == 0:
                    pool.wait_ge(part_done[2], 3 * b)
                pool.tensor_tensor(qk[:, 2 * i:2 * i + tiles, :].rearrange("p i t -> p (i t)"), roped_cos[:, 0:w],
                                   swapped[:, 0:w], ALU.add).then_inc(rope_done, 1)

            def v_third(b):
                pool.wait_ge(v_step, 3 * b + 2)
                pool.tensor_tensor(v_aug[:, b % V_RING, :, :, 2 * DH:3 * DH], v_rest[:, :, :, :],
                                   v_aug[:, b % V_RING, :, :, DH:2 * DH], ALU.subtract).then_inc(v_step, 1)

            def split_first(b, i):
                c = slice(2 * i, min(2 * i + 2, R + 1))
                pool.wait_ge(part_done[0], 3 * b + i + 1)
                pool.tensor_tensor(qk[:, c, :], qk[:, c, :], part[0][:, c, :], ALU.subtract).then_inc(rest_done, 1)

            def split_second(b, i):
                c = slice(2 * i, min(2 * i + 2, R + 1))
                pool.wait_ge(part_done[1], 3 * b + i + 1)
                pool.wait_ge(rest_done, 3 * b + i + 1)
                pool.tensor_tensor(part[2][:, c, :], qk[:, c, :], part[1][:, c, :], ALU.subtract).then_inc(part_done[2], 1)

            def mask(u):
                i = u % PROBS
                for c, width in ((0, S), (R * S, P)):
                    pool.wait_ge(exp_done, 2 * u + (2 if c else 1))
                    v = prob[:, i, c:c + R * width].rearrange("p (r q) -> p r q", r=R)[:, :, 0:P]
                    pool.affine_select(out=v, in_=v, compare_op=ALU.is_ge, fill=0.0, base=0,
                                       pattern=[[0, R], [1, P]], channel_multiplier=-1).then_inc(masked, 1)

            def second_part(u):
                i = u % 2
                c = slice(R * S, PCOLS)
                pool.wait_ge(p1_done, u + 1)
                pool.tensor_tensor(p2[:, i, c], prob[:, u % PROBS, c], p1[:, i, c], ALU.subtract).then_inc(p2_pool, 1)

            def scale(u):
                b, g = divmod(u, G)
                i = u % 2
                pool.wait_ge(o_evac, 2 * u + 2)
                if b and g == 0:
                    pool.wait_ge(turn_full, nth(("attnT", b - 1, NT - 1), TURN) + 1)
                dst = attn[:, :, g * R * DH:(g + 1) * R * DH].rearrange("p t (r d) -> p t r d", r=R)
                src = o_sum[:, i, :, :].rearrange("p (t r) d -> p t r d", t=NT)
                inv = o_inv[:, i, :].rearrange("p (t r) -> p t r", t=NT).unsqueeze(3).broadcast_to([P, NT, R, DH])
                pool.tensor_tensor(dst, src, inv, ALU.mult).then_inc(o_scaled, 1)

            def inverse_deviation(n, t):
                pool.wait_ge(stat_done, n + 1)
                link(pool.tensor_scalar(var_eps[:, t:t + 1], mean_var[:, t, 1:2], EPS, 0.0, ALU.add, ALU.add))
                link(pool.tensor_tensor(rstd[:, t:t + 1], var_eps[:, t:t + 1], half[:, t:t + 1], ALU.pow))
                pool.tensor_scalar(shift[:, t:t + 1], mean_var[:, t, 0:1], rstd[:, t:t + 1], -1.0, ALU.mult,
                                   ALU.mult).then_inc(rstd_done, 1)

            for i in range(3):
                split_second(0, i)
            v_third(0)
            for j in range(STEPS):
                if j < UNITS and 0 <= j - LAG_SPLIT:
                    second_part(j - LAG_SPLIT)
                for kind, b, t in dense_of(j - 1):
                    if kind in ("wo", "ffn"):
                        inverse_deviation(4 * b + t + (2 if kind == "ffn" else 0), t)
                if 0 <= j - LAG_ST < UNITS:
                    mask(j - LAG_ST)
                if j >= UNITS and j - LAG_SPLIT < UNITS:
                    second_part(j - LAG_SPLIT)
                for kind, b, t in dense_of(j - 2):
                    if kind == "wo":
                        pool.wait_ge(ln_done, 4 * b + t + 1)
                        pool.tensor_tensor(s_buf[:, t, :], y_buf[:, t, :], b_row[:, :], ALU.add).then_inc(yb_done, 1)
                for kind, b, t in dense_of(j - 2):
                    if kind == "qkv":
                        split_first(b, t)
                for kind, b, t in dense_of(j - 1):
                    if kind == "qkv":
                        qkv(b, t)
                if 0 <= j - LAG_GATHER < UNITS:
                    scale(j - LAG_GATHER)
                for kind, b, t in dense_of(j - 2):
                    if kind == "qkv":
                        split_second(b, t)
                        if t == 2:
                            v_third(b)


def kernel(L0_attn_x, L0_attn_w_qkv, L0_attn_w_o, L0_ffn_W_base, L0_ffn_b_base, L0_ffn_W_gate, L0_ffn_W_thr,
           L0_ffn_b_thr, L0_ffn_A_w, L0_ffn_B_w):
    import numpy as np
    import concourse.bacc as bacc
    from concourse.bass_utils import run_bass_kernel_spmd

    x = np.asarray(L0_attn_x)
    half_, freq, group = np.meshgrid(np.arange(2), np.arange(DH // 2), np.arange(G), indexing="ij")
    within = half_ * (DH // 2) + freq
    cols = [((R * group + r) * DH + within).ravel() for r in range(R)]
    cols += [(H * DH + group * DH + within).ravel(), np.arange(H * DH + G * DH, H * DH + 2 * G * DH)]
    cols = np.concatenate(cols)

    def chunked(w):
        return np.ascontiguousarray(w.T.reshape(KC, P, w.shape[0]).transpose(1, 0, 2))

    a_w = np.asarray(L0_ffn_A_w).reshape(E * LR, D)
    adapter = np.concatenate([a_w, np.asarray(L0_ffn_W_gate), np.asarray(L0_ffn_W_thr)[None],
                              np.zeros((1, D), np.float32)])
    inv_freq = (1.0 / 500000.0 ** (np.arange(0, DH, 2, dtype=np.float32) / np.float32(DH))).astype(np.float32)
    angle = np.outer(np.arange(S, dtype=np.float32), inv_freq).astype(np.float32)
    cos, sin = np.cos(angle), np.sin(angle)
    f = freq.ravel()
    sign = np.where(half_.ravel() == 0, -1.0, 1.0).astype(np.float32)
    tab = np.stack([cos[:, f].T, sin[:, f].T * sign[:, None]], axis=1).astype(np.float32)

    arrays = {
        "xT": np.ascontiguousarray(x.reshape(B, S, KC, P).transpose(0, 3, 2, 1)),
        "x": np.ascontiguousarray(x),
        "wqkv": chunked(np.asarray(L0_attn_w_qkv)[cols]),
        "wo": chunked(np.asarray(L0_attn_w_o)),
        "wb": chunked(np.asarray(L0_ffn_W_base)),
        "ag": chunked(adapter).reshape(P, KC * AG),
        "bw": np.ascontiguousarray(np.asarray(L0_ffn_B_w).transpose(0, 2, 1).reshape(E * LR, D)),
        "bbase": np.ascontiguousarray(np.broadcast_to(np.asarray(L0_ffn_b_base), (P, D))),
        "bthr": np.ascontiguousarray(np.broadcast_to(np.asarray(L0_ffn_b_thr), (P, 1))),
        "tab": np.ascontiguousarray(tab),
    }
    nc = bacc.Bacc("TRN2", target_bir_lowering=False, num_devices=1)
    aps = {n: nc.dram_tensor(f"in_{n}", a.shape, mybir.dt.from_np(a.dtype), kind="ExternalInput").ap()
           for n, a in arrays.items()}
    out = nc.dram_tensor("out", (B, S, D), F32, kind="ExternalOutput").ap()
    by_row = "b (t p) d -> b p t d"
    build(nc, aps["xT"], aps["x"].rearrange(by_row, p=P), aps["wqkv"], aps["wo"], aps["wb"], aps["ag"], aps["bw"],
          aps["bbase"], aps["bthr"], aps["tab"], out.rearrange(by_row, p=P))
    r = run_bass_kernel_spmd(nc, [{f"in_{n}": a for n, a in arrays.items()}], core_ids=[0])
    return r.results[0]["out"]
```
